# Optimizing a Trainium2 kernel written in Bass

```python
import numpy as np
import jax
import jax.numpy as jnp

def _softmax(x, axis=-1):
    return jax.nn.softmax(x, axis=axis)

def _gelu(x):
    return jax.nn.gelu(x, approximate=True)

def _silu(x):
    return jax.nn.silu(x)

def _sigmoid(x):
    return jax.nn.sigmoid(x)

def _layernorm(x, axis=-1, eps=1e-05):
    m = jnp.mean(x, axis=axis, keepdims=True)
    v = jnp.var(x, axis=axis, keepdims=True)
    return (x - m) / jnp.sqrt(v + eps)

def _scatter_add(tgt, idx, src, axis=0):
    return tgt.at[idx].add(src)

def _segment_sum(src, seg, n):
    return jax.ops.segment_sum(src, seg, n)
kernel_name = 'mk_gnn_resnorm_d4_gnn_r32_bca8dd'

def setup_inputs(seed: int=0):
    np.random.seed(seed)
    _w = jnp.asarray

    def _rec_inputs():
        import jax
        import jax.numpy as jnp
        _gk = jax.random.key(seed)
        x = -8.776e-05 + 1 * jax.random.normal(jax.random.fold_in(_gk, 1), (3125, 64), jnp.float32)
        src = jax.random.randint(jax.random.fold_in(_gk, 2), (100000,), 0, 3125, jnp.int32)
        dst = jax.random.randint(jax.random.fold_in(_gk, 3), (100000,), 0, 3125, jnp.int32)
        _o = jnp.argsort(dst, stable=True)
        src = src[_o]
        dst = dst[_o]
        edge_attr_64 = 7.68618e-05 + 1.00005 * jax.random.normal(jax.random.fold_in(_gk, 12), (100000, 64), jnp.float32)
        edge_type_16 = jax.random.randint(jax.random.fold_in(_gk, 14), (100000,), 0, 16, jnp.int32)
        edge_type_32 = jax.random.randint(jax.random.fold_in(_gk, 15), (100000,), 0, 32, jnp.int32)
        edge_weight = jax.random.uniform(jax.random.fold_in(_gk, 16), (100000,), jnp.float32, 0.0, 1)
        edge_weight1 = jax.random.uniform(jax.random.fold_in(_gk, 17), (100000, 1), jnp.float32, 0.0, 1)
        return (x, src, dst, edge_attr_64, edge_type_16, edge_type_32, edge_weight, edge_weight1)
    x, src, dst, edge_attr_64, edge_type_16, edge_type_32, edge_weight, edge_weight1 = _rec_inputs()

    def _L0_gnn_setup():
        import jax, jax.numpy as jnp
        import numpy as np
        N = 2500
        E = 40000
        D_IN = 64
        D_OUT = 64
        key = jax.random.key(seed)
        k1, k2, k3, k4 = jax.random.split(key, 4)
        features = jax.random.normal(k1, (N, D_IN), dtype=jnp.float32)
        src = jax.random.randint(k2, (E,), 0, N, dtype=jnp.int32)
        dst = jax.random.randint(k3, (E,), 0, N, dtype=jnp.int32)
        w = jnp.ones((E,), dtype=jnp.float32)
        W = jax.random.normal(k4, (D_OUT, D_IN), dtype=jnp.float32) / np.sqrt(D_IN)
        b = jnp.zeros((D_OUT,), dtype=jnp.float32)
        return {'features': features, 'src': src, 'dst': dst, 'w': w, 'W': W, 'b': b}
    _L0_gnn_all = _L0_gnn_setup()
    _L0_gnn_in = {k: v for k, v in _L0_gnn_all.items() if k in ('W', 'b')}
    del _L0_gnn_all

    def _L1_gnn_setup():
        import jax, jax.numpy as jnp
        import numpy as np
        N_NODES = 3125
        N_EDGES = 31250
        D_IN = 64
        D_OUT = 64
        key = jax.random.key(seed)
        k_x, k_ei, k_ea, k_w, k_b = jax.random.split(key, 5)
        x = jax.random.normal(k_x, (N_NODES, D_IN), dtype=jnp.float32)
        edge_index = jax.random.randint(k_ei, (2, N_EDGES), 0, N_NODES, dtype=jnp.int64)
        edge_attr = jax.random.normal(k_ea, (N_EDGES, D_IN), dtype=jnp.float32)
        bound = 1.0 / np.sqrt(D_IN)
        W = jax.random.uniform(k_w, (D_OUT, D_IN), dtype=jnp.float32, minval=-bound, maxval=bound)
        b = jax.random.uniform(k_b, (D_OUT,), dtype=jnp.float32, minval=-bound, maxval=bound)
        eps = jnp.zeros((), dtype=jnp.float32)
        return {'x': x, 'edge_index': edge_index, 'edge_attr': edge_attr, 'W': W, 'b': b, 'eps': eps}
    _L1_gnn_all = _L1_gnn_setup()
    _L1_gnn_in = {k: v for k, v in _L1_gnn_all.items() if k in ('W', 'b', 'eps')}
    del _L1_gnn_all

    def _L2_gnn_setup():
        import jax, jax.numpy as jnp
        import numpy as np
        N_NODES = 50000
        N_EDGES = 25000
        IN_F = 64
        OUT_F = 64
        N_REL = 32
        N_BASES = 30
        key = jax.random.key(seed)
        ks = jax.random.split(key, 6)
        x = jax.random.normal(ks[0], (N_NODES, IN_F), dtype=jnp.float32)
        edge_index = jax.random.randint(ks[1], (2, N_EDGES), 0, N_NODES, dtype=jnp.int64)
        edge_type = jax.random.randint(ks[2], (N_EDGES,), 0, N_REL, dtype=jnp.int64)
        basis = jax.random.normal(ks[3], (N_BASES, IN_F, OUT_F), dtype=jnp.float32) * 0.01
        coeff = jax.random.normal(ks[4], (N_REL, N_BASES), dtype=jnp.float32) * 0.01
        self_weight = jax.random.normal(ks[5], (IN_F, OUT_F), dtype=jnp.float32) * 0.01
        bias = jnp.zeros((OUT_F,), dtype=jnp.float32)
        return {'x': x, 'edge_index': edge_index, 'edge_type': edge_type, 'num_nodes': N_NODES, 'basis': basis, 'coeff': coeff, 'self_weight': self_weight, 'bias': bias}
    _L2_gnn_all = _L2_gnn_setup()
    _L2_gnn_in = {k: v for k, v in _L2_gnn_all.items() if k in ('basis', 'coeff', 'self_weight', 'bias')}
    del _L2_gnn_all

    def _L3_gnn_setup():
        import jax, jax.numpy as jnp
        import numpy as np
        N_NODES = 3125
        N_EDGES = 100000
        IN_FEAT = 64
        OUT_FEAT = 64
        NUM_RELS = 16
        key = jax.random.key(seed)
        k1, k2, k3, k4, k5, k6 = jax.random.split(key, 6)
        h = jax.random.normal(k1, (N_NODES, IN_FEAT), dtype=jnp.float32)
        weight = jax.random.normal(k2, (NUM_RELS, IN_FEAT, OUT_FEAT), dtype=jnp.float32) * 0.1
        norm = jax.random.uniform(k3, (N_EDGES, 1), dtype=jnp.float32)
        src = jax.random.randint(k4, (N_EDGES,), 0, N_NODES, dtype=jnp.int32)
        dst = jax.random.randint(k5, (N_EDGES,), 0, N_NODES, dtype=jnp.int32)
        rel_type = jax.random.randint(k6, (N_EDGES,), 0, NUM_RELS, dtype=jnp.int32)
        return {'h': h, 'weight': weight, 'norm': norm, 'src': src, 'dst': dst, 'rel_type': rel_type}
    _L3_gnn_all = _L3_gnn_setup()
    _L3_gnn_in = {k: v for k, v in _L3_gnn_all.items() if k in ('weight',)}
    del _L3_gnn_all
    return {'x': x, 'src': src, 'dst': dst, 'edge_attr_64': edge_attr_64, 'edge_type_16': edge_type_16, 'edge_type_32': edge_type_32, 'edge_weight': edge_weight, 'edge_weight1': edge_weight1, 'L0_gnn_W': _L0_gnn_in['W'], 'L0_gnn_b': _L0_gnn_in['b'], 'L1_gnn_W': _L1_gnn_in['W'], 'L1_gnn_b': _L1_gnn_in['b'], 'L1_gnn_eps': _L1_gnn_in['eps'], 'L2_gnn_basis': _L2_gnn_in['basis'], 'L2_gnn_coeff': _L2_gnn_in['coeff'], 'L2_gnn_self_weight': _L2_gnn_in['self_weight'], 'L2_gnn_bias': _L2_gnn_in['bias'], 'L3_gnn_weight': _L3_gnn_in['weight']}

def reference(x, src, dst, edge_attr_64, edge_type_16, edge_type_32, edge_weight, edge_weight1, L0_gnn_W, L0_gnn_b, L1_gnn_W, L1_gnn_b, L1_gnn_eps, L2_gnn_basis, L2_gnn_coeff, L2_gnn_self_weight, L2_gnn_bias, L3_gnn_weight):
    import jax
    import jax.numpy as jnp

    def _L0_gnn_ref(features, src, dst, w, W, b):
        import jax, jax.numpy as jnp
        import numpy as np
        N = 2500
        E = 40000
        D_IN = 64
        D_OUT = 64
        n = features.shape[0]
        ones = jnp.ones_like(w)
        in_deg = jax.ops.segment_sum(ones, dst, num_segments=n)
        out_deg = jax.ops.segment_sum(ones, src, num_segments=n)
        d_in = jax.lax.rsqrt(jnp.maximum(in_deg, 1.0))[:, None]
        d_out = jax.lax.rsqrt(jnp.maximum(out_deg, 1.0))[:, None]
        h = features * d_out
        m = h[src] * w[:, None]
        agg = jax.ops.segment_sum(m, dst, num_segments=n)
        h = agg * d_in
        return h @ W.T + b

    def _L1_gnn_ref(x, edge_index, edge_attr, W, b, eps):
        import jax, jax.numpy as jnp
        import numpy as np
        N_NODES = 3125
        N_EDGES = 31250
        D_IN = 64
        D_OUT = 64
        src = edge_index[0]
        dst = edge_index[1]
        msg = jax.nn.relu(x[src] + edge_attr)
        agg = jax.ops.segment_sum(msg, dst, num_segments=x.shape[0])
        h = (1.0 + eps) * x + agg
        out = h @ W.T + b
        return jax.nn.relu(out)

    def _L2_gnn_ref(x, edge_index, edge_type, num_nodes, basis, coeff, self_weight, bias):
        import jax, jax.numpy as jnp
        import numpy as np
        N_NODES = 50000
        N_EDGES = 25000
        IN_F = 64
        OUT_F = 64
        N_REL = 32
        N_BASES = 30
        rel_weight = jnp.einsum('rb,bio->rio', coeff, basis)
        source_idx = edge_index[0]
        target_idx = edge_index[1]
        src_feats = x[source_idx]

        def body(out, rw_r):
            rw, r = rw_r
            mask = (edge_type == r).astype(jnp.float32)
            msg = src_feats @ rw * mask[:, None]
            return (out.at[target_idx].add(msg), None)
        out0 = jnp.zeros((num_nodes, rel_weight.shape[-1]), dtype=jnp.float32)
        out, _ = jax.lax.scan(body, out0, (rel_weight, jnp.arange(rel_weight.shape[0])))
        in_degree = jnp.zeros((num_nodes,), dtype=jnp.float32).at[target_idx].add(1.0)
        in_degree = jnp.maximum(in_degree, 1.0)
        out = out / in_degree[:, None]
        out = out + x @ self_weight + bias
        return out

    def _L3_gnn_ref(h, weight, norm, src, dst, rel_type):
        import jax, jax.numpy as jnp
        import numpy as np
        N_NODES = 3125
        N_EDGES = 100000
        IN_FEAT = 64
        OUT_FEAT = 64
        NUM_RELS = 16
        n_nodes = h.shape[0]
        transformed = jnp.einsum('nd,rdo->nro', h, weight)
        msg = transformed[src, rel_type] * norm
        agg = jax.ops.segment_sum(msg, dst, num_segments=n_nodes)
        return jax.nn.relu(agg)
    edge_index = jnp.stack([src, dst])
    x = _layernorm(x + _L0_gnn_ref(x, src, dst, edge_weight, L0_gnn_W, L0_gnn_b), axis=-1)
    x = _layernorm(x + _L1_gnn_ref(x, edge_index, edge_attr_64, L1_gnn_W, L1_gnn_b, L1_gnn_eps), axis=-1)
    x = _layernorm(x + _L2_gnn_ref(x, edge_index, edge_type_32, 3125, L2_gnn_basis, L2_gnn_coeff, L2_gnn_self_weight, L2_gnn_bias), axis=-1)
    x = _layernorm(x + _L3_gnn_ref(x, L3_gnn_weight, edge_weight1, src, dst, edge_type_16), axis=-1)
    return x

_drawn_inputs = setup_inputs


def setup_inputs(seed=0):
    import zlib

    import numpy as np

    out = dict(_drawn_inputs(seed))
    spreads = {'L0_gnn_b': (0.0, 0.1), 'L2_gnn_bias': (0.0, 0.1)}
    factors = {'edge_weight': 3.651, 'L1_gnn_b': 5.275, 'L2_gnn_basis': 8.0, 'L2_gnn_coeff': 8.0}
    for name, (base, spread) in spreads.items():
        noise = np.random.default_rng([zlib.crc32(name.encode()), seed]).standard_normal(out[name].shape)
        drawn = base * np.exp(spread * noise) if base else spread * noise
        out[name] = jnp.asarray(drawn.astype(out[name].dtype))
    for name, factor in factors.items():
        out[name] = (out[name] * factor).astype(out[name].dtype)
    return out
```

```python
import concourse.bass as bass
from concourse import mybir
from contextlib import ExitStack


def gnn_stack(nc, x, src, dst, edge_attr, etype16, etype32, weight0, weight3,
              W0, b0, W1, b1, eps1, basis, coeff, self_w, b2, W3, out):
    fp32, bf16, i32 = mybir.dt.float32, mybir.dt.bfloat16, mybir.dt.int32
    ALU, ACT, AX = mybir.AluOpType, mybir.ActivationFunctionType, mybir.AxisListType

    P = 128
    N, D = x.shape
    E = src.shape[0]
    R2, NB = coeff.shape
    R3 = W3.shape[0]
    HALF = P // 2
    SLOTS = -(-E // P)
    E_HALF = HALF * SLOTS
    HI0 = E - E_HALF
    OVERLAP = E_HALF - HI0
    C = 23
    PAIRS = SLOTS // (2 * C)
    assert PAIRS * 2 * C == SLOTS
    COLS = -(-N // P)
    NPAD = COLS * P
    LASTROWS = N - (COLS - 1) * P
    G = 5
    NG = COLS // G
    GW = G * D
    HC = 2 * COLS
    HCH = COLS
    LN_EPS = 1e-5
    BANK = 512
    PER_CHUNK = 16 * C
    INITS = 9
    INEXACT = dict(allow_small_or_imprecise_dtypes=True)

    def stored(n, y):
        return (n + 1 - y) // 2

    assert NG * G == COLS and COLS == 25

    def dram(name, shape):
        return nc.dram_tensor(name, shape, fp32, kind="Internal").ap()

    table0 = dram("table0", [NPAD, D])
    table1 = dram("table1", [NPAD, D])
    table2 = dram("table2", [NPAD * R2, D])
    table3 = dram("table3", [NPAD * R3, D])
    sums = dram("running_sums", [P * SLOTS, D])
    tables = [table0, table1, table2, table3]
    sums_pt = sums.rearrange("(p t) f -> p (t f)", t=SLOTS)

    def by_col(table):
        return table.rearrange("(c p) f -> p c f", p=P)

    def halves(vec):
        return (vec[0:E_HALF].rearrange("(p t) -> p t", t=SLOTS),
                vec[HI0:E].rearrange("(p t) -> p t", t=SLOTS))

    attr_lo = edge_attr[0:E_HALF, :].rearrange("(p t) f -> p (t f)", t=SLOTS)
    attr_hi = edge_attr[HI0:E, :].rearrange("(p t) f -> p (t f)", t=SLOTS)

    ctx = ExitStack()
    with ctx:
        def sb(name, shape, dt=fp32):
            return ctx.enter_context(nc.sbuf_tensor(name, shape, dt))

        def sem(name):
            return ctx.enter_context(nc.semaphore(name))

        src_i = sb("src_i", [P, SLOTS + 2 * C], i32)
        dst_i = sb("dst_i", [P, SLOTS], i32)
        rows2 = sb("rows2", [P, SLOTS + 2 * C], i32)
        rows3 = sb("rows3", [P, SLOTS + 2 * C], i32)
        key_i = sb("key_i", [P, SLOTS], i32)
        src_lo, src_hi, dst_lo, dst_hi = (sb(n, [P, SLOTS], bf16) for n in ("src_lo", "src_hi", "dst_lo", "dst_hi"))
        w0_sb = sb("w0_sb", [P, SLOTS])
        w3_sb = sb("w3_sb", [P, SLOTS])
        same = sb("same", [P, SLOTS])
        idx = [sb(f"idx{b}", [P, C], i32) for b in range(2)]
        got = [sb(f"got{b}", [P, C * D]) for b in range(2)]
        attr = [sb(f"attr{b}", [P, C * D]) for b in range(2)]
        msgT = [sb(f"msgT{b}", [P, D, C]) for b in range(2)]
        keep = [sb(f"keep{b}", [P, D, C], bf16) for b in range(2)]
        run = [sb(f"run{b}", [P, C * D]) for b in range(2)]
        hot_lo = [sb(f"hot_lo{b}", [P, C, HALF], bf16) for b in range(2)]
        hot_hi = [sb(f"hot_hi{b}", [P, C, HC], bf16) for b in range(2)]
        ramp_f = sb("ramp_f", [P, P])
        ramp_lo = sb("ramp_lo", [P, HALF], bf16)
        ramp_hi = sb("ramp_hi", [P, HC], bf16)
        part_f = sb("part_f", [P, 1])
        ident = sb("ident", [P, P])
        upper = sb("upper", [P, P])
        ones = sb("ones", [P, P])
        zero_b = sb("zero_b", [P, HALF], bf16)
        feats = sb("feats", [P, COLS, D])
        scaled = sb("scaled", [P, COLS, D])
        xT = sb("xT", [D, NPAD])
        aggT = [sb(f"aggT{b}", [D, G * P]) for b in range(2)]
        ends_sum = sb("ends_sum", [P, COLS, D])
        tail_sum = sb("tail_sum", [P, D])
        carry_hot = sb("carry_hot", [P, NPAD])
        next_i = sb("next_i", [P, 1], i32)
        last_dst, goes_on, eps_sb, eps1p = (sb(n, [P, 1]) for n in ("last_dst", "goes_on", "eps_sb", "eps1p"))
        (deg_out, out_sqrt, out_scale, deg_in, has_in, in_clip, in_sqrt, in_scale, in_inv, col_tot, col_cum,
         end_f, end_up) = (sb(n, [P, COLS]) for n in (
             "deg_out", "out_sqrt", "out_scale", "deg_in", "has_in", "in_clip", "in_sqrt", "in_scale",
             "in_inv", "col_tot", "col_cum", "end_f", "end_up"))
        end_i = sb("end_i", [P, COLS], i32)
        ta = sb("ta", [P, GW])
        tb = sb("tb", [P, GW])
        agg = [sb(f"agg{b}", [P, GW]) for b in range(2)]
        row_sum, row_mean, row_sq, row_var, row_std, row_inv = (
            sb(n, [P, G]) for n in ("row_sum", "row_mean", "row_sq", "row_var", "row_std", "row_inv"))
        w_raw = sb("w_raw", [D, 2, D])
        wT = sb("wT", [D, 2, D])
        sw_sb = sb("sw_sb", [D, D])
        bias = [sb(f"bias{l}", [P, D]) for l in range(3)]
        coeff_sb = sb("coeff_sb", [R2, NB])
        coeffT = sb("coeffT", [NB, R2])
        basis_sb = sb("basis_sb", [NB, D * D])
        rel2 = sb("rel2", [D, R2 * D])
        rel3 = sb("rel3", [D, R3 * D])
        ytile = [sb(f"ytile{b}", [P, R2 * D]) for b in range(2)]

        psA = ctx.enter_context(nc.psum_tensor("psA", [P, 4 * BANK], fp32))
        psB = ctx.enter_context(nc.psum_tensor("psB", [P, 4 * BANK], fp32))
        ps = [psA, psB]
        hist = [psA[:, 0:HCH], psA[:, BANK:BANK + HCH]]
        cum_ps = psA[:, 2 * BANK:2 * BANK + COLS]
        tot_ps = psA[:, 3 * BANK:3 * BANK + COLS]

        def carry_ps(q):
            return psA[:, (q % 2) * BANK:(q % 2) * BANK + GW]

        def lin_ps(q):
            return psA[:, (2 + q % 2) * BANK:(2 + q % 2) * BANK + GW]

        def turn_ps(q):
            return psB[0:D, (q % 2) * 2 * BANK:(q % 2) * 2 * BANK + G * P]

        def over_cols(v, n):
            return v.unsqueeze(2).broadcast_to([P, n, D])

        def cube(t):
            return t.rearrange("p (c f) -> p c f", f=D)

        s_init = sem("buffers_cleared")
        s_src, s_dst, s_typ, s_w, s_x, s_par = (
            sem(n) for n in ("src_loaded", "dst_loaded", "types_loaded", "weights_loaded", "x_loaded",
                             "params_loaded"))
        s_pool = sem("ramps_made")
        s_v = sem("vector_steps")
        s_const = sem("consts_ready")
        s_same = sem("segment_flags_ready")
        s_hot = [sem(f"hot_made{b}") for b in range(2)]
        s_cnt = [sem(f"hot_counted{b}") for b in range(2)]
        s_deg = sem("degrees_counted")
        s_clip = sem("degrees_clipped")
        s_sqrt = sem("degree_sqrt_done")
        s_cum = sem("columns_summed")
        s_table = sem("table_stored")
        s_scaled = sem("scaled_ready")
        s_idx = [sem(f"idx_staged{b}") for b in range(2)]
        s_got = [sem(f"rows_gathered{b}") for b in range(2)]
        s_used = [sem(f"rows_used{b}") for b in range(2)]
        s_attr = [sem(f"attr_loaded{b}") for b in range(2)]
        s_relu = [sem(f"attr_used{b}") for b in range(2)]
        s_mixed = sem("chunk_carried")
        s_keep = [sem(f"keep_spread{b}") for b in range(2)]
        s_scan = [sem(f"chunk_scanned{b}") for b in range(2)]
        s_run = [sem(f"sums_copied{b}") for b in range(2)]
        s_wr = [sem(f"sums_stored{b}") for b in range(2)]
        s_endi = sem("end_rows_ready")
        s_end = [sem(f"ends_gathered{g}") for g in range(NG)]
        s_tail = sem("tail_ready")
        s_carry = sem("carry_multiplied")
        s_agg = sem("agg_ready")
        s_turn = sem("agg_transposed")
        s_aggT = sem("aggT_copied")
        s_lin = sem("linear_done")
        s_var = sem("variance_ready")
        s_std = sem("std_ready")
        s_new = sem("features_ready")
        s_xt = sem("x_transposed")
        s_xT = sem("xT_copied")
        s_wt = sem("weights_multiplied")
        s_wc = sem("weights_copied")
        s_y = sem("table_product")
        s_yc = [sem("table_copied_act"), sem("table_copied_vec")]
        s_yst = [sem(f"wide_table_stored{b}") for b in range(2)]
        s_out = sem("output_stored")
        s_go = sem("chunk_started")

        LAYER_ROWS = [src_i, src_i, rows2, rows3]
        WIDE = {2: (R2, 0), 3: (R3, COLS)}

        def trips(eng, layer, body):
            if layer == 0:
                body(0)
            with eng.Fori(1 if layer == 0 else 0, PAIRS) as trip:
                body(trip)

        def first(layer, trip):
            return layer == 0 and isinstance(trip, int)

        block = ctx.enter_context(nc.Block())

        @block.sync
        def _(sp):
            sp.wait_ge(s_init, INITS)
            for n, h in enumerate(halves(src)):
                sp.dma_start(src_i[n * HALF:(n + 1) * HALF, 0:SLOTS], h).then_inc(s_src, 16)
            sp.dma_start(feats[:, 0:COLS - 1, :], by_col(x[0:(COLS - 1) * P, :])).then_inc(s_x, 16)
            sp.dma_start(feats[0:LASTROWS, COLS - 1, :], x[(COLS - 1) * P:N, :]).then_inc(s_x, 16)
            for n, h in enumerate(halves(dst)):
                sp.dma_start(dst_i[n * HALF:(n + 1) * HALF, :], h).then_inc(s_dst, 16)
            after = dst[SLOTS:SLOTS + E_HALF].rearrange("(p t) -> p t", t=SLOTS)
            sp.dma_start(next_i[0:HALF, :], after[:, 0:1], allow_slow_non_contiguous=True).then_inc(s_dst, 16)
            after = dst[HI0 + SLOTS:E].rearrange("(p t) -> p t", t=SLOTS)
            sp.dma_start(next_i[HALF:P - 1, :], after[:, 0:1], allow_slow_non_contiguous=True).then_inc(s_dst, 16)
            for v, t in ((weight0, w0_sb), (weight3.rearrange("e o -> (e o)"), w3_sb)):
                for n, h in enumerate(halves(v)):
                    sp.dma_start(t[n * HALF:(n + 1) * HALF, :], h).then_inc(s_w, 16)
            for v, t in ((etype32, rows2), (etype16, rows3)):
                for n, h in enumerate(halves(v)):
                    sp.dma_start(t[n * HALF:(n + 1) * HALF, 0:SLOTS], h).then_inc(s_typ, 16)

            def store_sums(layer):
                def load_attr(b, at):
                    for n, half in enumerate((attr_lo, attr_hi)):
                        sp.dma_start(attr[b][n * HALF:(n + 1) * HALF, :],
                                     half[:, bass.ds(at, C * D)]).then_inc(s_attr[b], 16)

                def body(trip, last=False):
                    for b in range(2):
                        sp.wait_ge(s_run[b], layer * PAIRS + 1 + trip)
                        sp.dma_start(sums_pt[:, bass.ds(trip * (2 * C * D) + b * C * D, C * D)],
                                     run[b][:, :]).then_inc(s_wr[b], 16)
                        if layer == 1 and not last:
                            load_attr(b, trip * (2 * C * D) + (2 + b) * C * D)

                if layer == 1:
                    for b in range(2):
                        load_attr(b, b * C * D)
                with sp.Fori(0, PAIRS - 1) as trip:
                    body(trip)
                body(PAIRS - 1, last=True)

            def store_table(layer):
                if layer < 2:
                    for g in range(NG):
                        sp.wait_ge(*((s_scaled, g + 1) if layer == 0 else (s_new, g + 1)))
                        t = scaled if layer == 0 else feats
                        sp.dma_start(by_col(tables[layer])[:, g * G:(g + 1) * G, :],
                                     t[:, g * G:(g + 1) * G, :]).then_inc(s_table, 16)
                    return
                rel, before = WIDE[layer]
                wide = tables[layer].rearrange("(n r) f -> n (r f)", r=rel)
                for c in range(COLS):
                    for s in s_yc:
                        sp.wait_ge(s, before + c + 1)
                    y = (before + c) % 2
                    sp.dma_start(wide[c * P:(c + 1) * P, :], ytile[y][:, 0:rel * D]).then_inc(s_yst[y], 16)

            for layer in range(4):
                store_table(layer)
                store_sums(layer)
            sp.wait_ge(s_new, 4 * NG)
            sp.dma_start(by_col(out[0:(COLS - 1) * P, :]), feats[:, 0:COLS - 1, :]).then_inc(s_out, 16)
            sp.dma_start(out[(COLS - 1) * P:N, :], feats[0:LASTROWS, COLS - 1, :]).then_inc(s_out, 16)
            sp.wait_ge(s_out, 32)

        @block.gpsimd
        def _(pool):
            made = [
                nc.gpsimd.iota(ramp_f[:, :], pattern=[[1, P]], base=0, channel_multiplier=0, **INEXACT),
                nc.gpsimd.iota(part_f[:, :], pattern=[[0, 1]], base=0, channel_multiplier=1, **INEXACT),
                nc.gpsimd.iota(ramp_lo[:, :], pattern=[[1, HALF]], base=0, channel_multiplier=0, **INEXACT),
                nc.gpsimd.iota(ramp_hi[:, :], pattern=[[1, 2], [2, HCH]], base=0, channel_multiplier=0, **INEXACT),
                nc.gpsimd.iota(carry_hot[:, :], pattern=[[1, NPAD]], base=0, channel_multiplier=0, **INEXACT),
                nc.gpsimd.memset(ones[:, :], 1.0),
            ]
            for ins in made:
                ins.then_inc(s_pool, 1)

            def gather_edges(layer):
                if layer < 2:
                    pool.wait_ge(s_table, 16 * NG * (layer + 1))
                else:
                    for y in range(2):
                        pool.wait_ge(s_yst[y], 16 * stored(WIDE[layer][1] + COLS, y))

                def body(trip):
                    for b in range(2):
                        pool.wait_ge(s_idx[b], layer * (PAIRS + 1) + 1 + trip)
                        if not first(layer, trip):
                            pool.wait_ge(s_used[b], layer * PAIRS + trip)
                        pool.sem_inc(s_go, 1)
                        for s in range(C):
                            nc.gpsimd.indirect_dma_start(
                                out=got[b][:, s * D:(s + 1) * D], out_offset=None, in_=tables[layer],
                                in_offset=bass.IndirectOffsetOnAxis(ap=idx[b][:, s:s + 1], axis=0),
                            ).then_inc(s_got[b], 16)

                trips(pool, layer, body)

            def gather_ends(layer):
                for b in range(2):
                    pool.wait_ge(s_wr[b], 16 * PAIRS * (layer + 1))
                pool.wait_ge(s_endi, 1)
                if layer:
                    pool.wait_ge(s_agg, NG * layer)
                for c in range(COLS):
                    nc.gpsimd.indirect_dma_start(
                        out=ends_sum[:, c, :], out_offset=None, in_=sums,
                        in_offset=bass.IndirectOffsetOnAxis(ap=end_i[:, c:c + 1], axis=0),
                    ).then_inc(s_end[c // G], 16)

            for layer in range(4):
                gather_edges(layer)
                gather_ends(layer)

        @block.scalar
        def _(act):
            act.wait_ge(s_init, INITS)
            act.dma_start(w_raw[:, 0, :], W0).then_inc(s_par, 16)
            act.dma_start(w_raw[:, 1, :], W1).then_inc(s_par, 16)
            act.dma_start(sw_sb[:, :], self_w).then_inc(s_par, 16)
            for t, v in zip(bias, (b0, b1, b2)):
                act.dma_start(t[:, :], v.unsqueeze(0).broadcast_to([P, D])).then_inc(s_par, 16)
            act.dma_start(eps_sb[:, :], eps1.unsqueeze(0).broadcast_to([P, 1])).then_inc(s_par, 16)
            act.dma_start(coeff_sb[:, :], coeff).then_inc(s_par, 16)
            act.dma_start(basis_sb[:, :], basis.rearrange("b i o -> b (i o)")).then_inc(s_par, 16)
            act.dma_start(rel3[:, :].rearrange("i (r o) -> i r o", r=R3),
                          W3.rearrange("r i o -> i r o")).then_inc(s_par, 16)
            act.wait_ge(s_clip, 1)
            nc.scalar.activation(out_sqrt[:, :], deg_out[:, :], ACT.Sqrt).then_inc(s_sqrt, 1)
            act.wait_ge(s_wt, 1)
            nc.scalar.copy(wT[:, :, :], psB[0:D, 0:2 * D].rearrange("i (l o) -> i l o", l=2)).then_inc(s_wc, 1)
            nc.scalar.copy(coeffT[:, :], psB[0:NB, BANK:BANK + R2]).then_inc(s_wc, 1)
            act.wait_ge(s_wt, 2)
            nc.scalar.copy(rel2[:, :].rearrange("i (r o) -> i o r", r=R2),
                           psB[0:D, :].rearrange("i (o r) -> i o r", r=R2)).then_inc(s_wc, 1)
            act.wait_ge(s_same, 3)

            def chunks(layer):
                def body(trip):
                    n = layer * PAIRS + trip
                    for b in range(2):
                        if not first(layer, trip):
                            act.wait_ge(s_scan[b], n)
                        nc.scalar.copy(keep[b][:, :, 1:C],
                                       same[:, bass.ds(trip * (2 * C) + b * C + 1, C - 1)]
                                       .unsqueeze(1).broadcast_to([P, D, C - 1])).then_inc(s_keep[b], 1)
                    for b in range(2):
                        act.wait_ge(s_scan[b], n + 1)
                        if not first(layer, trip):
                            act.wait_ge(s_wr[b], n * 16)
                        nc.scalar.copy(run[b][:, :].rearrange("p (t f) -> p f t", f=D),
                                       msgT[b][:, :, :]).then_inc(s_run[b], 1)

                trips(act, layer, body)

            def nodes(layer):
                if layer == 0:
                    act.wait_ge(s_clip, 2)
                    nc.scalar.activation(in_sqrt[:, :], in_clip[:, :], ACT.Sqrt).then_inc(s_sqrt, 1)

                def finish(g):
                    q = layer * NG + g
                    act.wait_ge(s_var, q + 1)
                    nc.scalar.activation(row_std[:, :], row_var[:, :], ACT.Sqrt).then_inc(s_std, 1)
                    if layer in (1, 2):
                        act.wait_ge(s_xt, q - NG + 1)
                        nc.scalar.copy(xT[:, g * G * P:(g + 1) * G * P], turn_ps(q)).then_inc(s_xT, 1)

                for g in range(NG):
                    q = layer * NG + g
                    if layer < 2:
                        act.wait_ge(s_turn, q + 1)
                        if q >= 2:
                            act.wait_ge(s_lin, q - 1)
                        nc.scalar.copy(aggT[q % 2][:, :], turn_ps(q)).then_inc(s_aggT, 1)
                    if g:
                        finish(g - 1)
                finish(NG - 1)

            def table(layer):
                rel, before = WIDE[layer]
                for c in range(COLS):
                    n = before + c
                    act.wait_ge(s_y, n + 1)
                    if n >= 2:
                        act.wait_ge(s_yst[n % 2], 16 * stored(n, n % 2))
                    nc.scalar.copy(ytile[n % 2][:, 0:rel * D // 2], ps[n % 2][:, 0:rel * D // 2])\
                        .then_inc(s_yc[0], 1)

            for layer in range(4):
                if layer >= 2:
                    table(layer)
                chunks(layer)
                nodes(layer)

        @block.tensor
        def _(pe):
            def count(which, base, trip):
                for b in range(2):
                    pe.wait_ge(s_hot[b], 2 * (base + trip) + 2)
                    for s in range(C):
                        for h in range(2):
                            last = nc.tensor.matmul(hist[which][h * HALF:(h + 1) * HALF, :], hot_lo[b][:, s, :],
                                                    hot_hi[b][:, s, h * HCH:(h + 1) * HCH],
                                                    start=False, stop=False, skip_group_check=True)
                    last.then_inc(s_cnt[b], 1)

            def bound(which, start):
                for h in range(2):
                    last = nc.tensor.matmul(hist[which][h * HALF:(h + 1) * HALF, :], zero_b[:, :],
                                            zero_b[:, 0:HCH], start=start, stop=not start,
                                            skip_group_check=True)
                if not start:
                    last.then_inc(s_deg, 1)

            pe.wait_ge(s_init, INITS)
            bound(0, True)
            bound(1, True)
            with pe.Fori(0, PAIRS) as trip:
                count(0, 0, trip)
            bound(0, False)
            pe.wait_ge(s_par, 16 * 10)
            pe.wait_ge(s_const, 1)
            for l in range(2):
                nc.tensor.transpose(psB[0:D, l * D:(l + 1) * D], w_raw[:, l, :], ident[0:D, 0:D])
            nc.tensor.transpose(psB[0:NB, BANK:BANK + R2], coeff_sb[:, :], ident[0:R2, 0:R2]).then_inc(s_wt, 1)
            pe.wait_ge(s_wc, 2)
            for o in range(D):
                last = nc.tensor.matmul(psB[0:D, o * R2:(o + 1) * R2], basis_sb[:, o:D * D:D], coeffT[:, :],
                                        start=True, stop=True)
            last.then_inc(s_wt, 1)
            with pe.Fori(0, PAIRS) as trip:
                count(1, PAIRS, trip)
            bound(1, False)
            pe.wait_ge(s_clip, 2)
            nc.tensor.matmul(cum_ps, upper[:, :], deg_in[:, :], start=True, stop=True)
            nc.tensor.matmul(tot_ps, ones[:, :], deg_in[:, :], start=True, stop=True).then_inc(s_cum, 1)

            def nodes(layer):
                def carry(g):
                    q = layer * NG + g
                    if g == 0:
                        pe.wait_ge(s_tail, layer + 1)
                        if layer == 0:
                            pe.wait_ge(s_endi, 1)
                    if q >= 2:
                        pe.wait_ge(s_agg, q - 1)
                    for j in range(G):
                        c = g * G + j
                        last = nc.tensor.matmul(carry_ps(q)[:, j * D:(j + 1) * D], carry_hot[:, c * P:(c + 1) * P],
                                                tail_sum[:, :], start=True, stop=True)
                    last.then_inc(s_carry, 1)

                def turn(q, source, done):
                    for j in range(G):
                        last = nc.tensor.transpose(turn_ps(q)[:, j * P:(j + 1) * P], source[:, j, :], ident[:, :])
                    last.then_inc(done, 1)

                def turn_new(g):
                    q = layer * NG + g
                    pe.wait_ge(s_new, q + 1)
                    if layer == 2 and g >= 2:
                        pe.wait_ge(s_xT, q - NG - 1)
                    turn(q, feats[:, g * G:(g + 1) * G, :], s_xt)

                if layer >= 2:
                    for s in s_yc:
                        pe.wait_ge(s, WIDE[layer][1] + COLS)
                carry(0)
                carry(1)
                for g in range(NG):
                    q = layer * NG + g
                    if layer < 2:
                        pe.wait_ge(s_agg, q + 1)
                        if layer == 0 and g == 0:
                            pe.wait_ge(s_wc, 3)
                        if q >= 2:
                            pe.wait_ge(s_aggT, q - 1)
                        if layer == 1 and g >= 2:
                            pe.wait_ge(s_xT, q - NG - 1)
                        turn(q, cube(agg[q % 2][:, :]), s_turn)
                        pe.wait_ge(s_aggT, q + 1)
                    if layer < 3:
                        if q >= 2:
                            pe.wait_ge(s_new, q - 1)
                        for j in range(G):
                            c = g * G + j
                            lhsT = aggT[q % 2][:, j * P:(j + 1) * P] if layer < 2 else xT[:, c * P:(c + 1) * P]
                            last = nc.tensor.matmul(lin_ps(q)[:, j * D:(j + 1) * D], lhsT,
                                                    wT[:, layer, :] if layer < 2 else sw_sb[:, :],
                                                    start=True, stop=True)
                        last.then_inc(s_lin, 1)
                    if g + 2 < NG:
                        carry(g + 2)
                    if layer in (1, 2) and g:
                        turn_new(g - 1)
                if layer in (1, 2):
                    turn_new(NG - 1)

            def table(layer):
                rel, before = WIDE[layer]
                w = rel2 if layer == 2 else rel3
                pe.wait_ge(s_xT, NG * (layer - 1))
                for c in range(COLS):
                    n = before + c
                    if c >= 2:
                        for s in s_yc:
                            pe.wait_ge(s, n - 1)
                    for k in range(rel * D // BANK):
                        last = nc.tensor.matmul(ps[n % 2][:, k * BANK:(k + 1) * BANK], xT[:, c * P:(c + 1) * P],
                                                w[:, k * BANK:(k + 1) * BANK], start=True, stop=True)
                    last.then_inc(s_y, 1)

            for layer in range(4):
                if layer >= 2:
                    table(layer)
                nodes(layer)

        @block.vector
        def _(v):
            steps = [0]

            def link(ins):
                steps[0] += 1
                ins.then_inc(s_v, 1)
                v.wait_ge(s_v, steps[0])

            for t, value in ((src_i[:, SLOTS:], 0), (rows2[:, SLOTS:], 0), (rows3[:, SLOTS:], 0),
                             (feats[:, COLS - 1, :], 0.0), (next_i[:, :], -1), (zero_b[:, :], 0.0),
                             (msgT[1][:, :, C - 1], 0.0), (keep[0][:, :, 0], 0.0), (keep[1][:, :, 0], 0.0)):
                nc.vector.memset(t, value).then_inc(s_init, 1)

            def split(nodes, lo, hi):
                link(nc.vector.tensor_scalar(key_i[:, :], nodes, HALF - 1, None, ALU.bitwise_and))
                link(nc.vector.tensor_copy(lo[:, :], key_i[:, :]))
                link(nc.vector.memset(lo[HALF:HALF + 1, 0:OVERLAP], -1.0))
                link(nc.vector.tensor_scalar(key_i[:, :], nodes, HALF.bit_length() - 1, None,
                                             ALU.logical_shift_right))
                link(nc.vector.tensor_copy(hi[:, :], key_i[:, :]))

            def hot(base, trip, b, lo, hi):
                if not (base == 0 and isinstance(trip, int)):
                    v.wait_ge(s_cnt[b], base + trip)
                at = bass.ds(trip * (2 * C) + b * C, C)
                for t, ramp, part, w in ((hot_lo, ramp_lo, lo, HALF), (hot_hi, ramp_hi, hi, HC)):
                    nc.vector.tensor_tensor(t[b][:, :, :], ramp[:, :].unsqueeze(1).broadcast_to([P, C, w]),
                                            part[:, at].unsqueeze(2).broadcast_to([P, C, w]),
                                            ALU.is_equal).then_inc(s_hot[b], 1)

            v.wait_ge(s_pool, 6)
            v.wait_ge(s_src, 32)
            split(src_i[:, 0:SLOTS], src_lo, src_hi)
            for b in range(2):
                hot(0, 0, b, src_lo, src_hi)
            with v.Fori(1, PAIRS) as trip:
                for b in range(2):
                    hot(0, trip, b, src_lo, src_hi)
            v.wait_ge(s_deg, 1)
            nc.vector.tensor_scalar(deg_out[:, :], hist[0], 1.0, None, ALU.max).then_inc(s_clip, 1)

            def stage(layer, b):
                nc.vector.tensor_copy(idx[b][:, :], LAYER_ROWS[layer][:, b * C:(b + 1) * C]).then_inc(s_idx[b], 1)

            stage(0, 0)
            stage(0, 1)
            v.wait_ge(s_sqrt, 1)
            link(nc.vector.reciprocal(out_scale[:, :], out_sqrt[:, :]))
            v.wait_ge(s_x, 32)
            for g in range(NG):
                cols = slice(g * G, (g + 1) * G)
                nc.vector.tensor_tensor(scaled[:, cols, :], feats[:, cols, :], over_cols(out_scale[:, cols], G),
                                        ALU.mult).then_inc(s_scaled, 1)
            v.wait_ge(s_dst, 64)
            nc.vector.tensor_tensor(same[:, 1:SLOTS], dst_i[:, 1:SLOTS], dst_i[:, 0:SLOTS - 1],
                                    ALU.is_equal).then_inc(s_same, 1)
            nc.vector.memset(same[:, 0:1], 0.0).then_inc(s_same, 1)
            v.wait_ge(s_same, 2)
            nc.vector.memset(same[HALF:HALF + 1, OVERLAP:OVERLAP + 1], 0.0).then_inc(s_same, 1)
            link(nc.vector.tensor_copy(last_dst[:, :], dst_i[:, SLOTS - 1:SLOTS]))
            link(nc.vector.tensor_tensor(goes_on[:, :], next_i[:, :], last_dst[:, :], ALU.is_equal))
            link(nc.vector.tensor_scalar(carry_hot[:, :], carry_hot[:, :], last_dst[:, 0:1], goes_on[:, 0:1],
                                         ALU.is_equal, ALU.mult))
            link(nc.vector.tensor_scalar(upper[:, :], ramp_f[:, :], part_f[:, 0:1], None, ALU.is_ge))
            nc.vector.tensor_scalar(ident[:, :], ramp_f[:, :], part_f[:, 0:1], None, ALU.is_equal).then_inc(s_const, 1)
            split(dst_i[:, :], dst_lo, dst_hi)
            v.wait_ge(s_typ, 64)
            for rows, rel in ((rows2, R2), (rows3, R3)):
                link(nc.vector.tensor_scalar(key_i[:, :], src_i[:, 0:SLOTS], rel.bit_length() - 1, None,
                                             ALU.logical_shift_left))
                link(nc.vector.tensor_tensor(rows[:, 0:SLOTS], rows[:, 0:SLOTS], key_i[:, :], ALU.add))
            v.wait_ge(s_par, 16 * 10)
            link(nc.vector.tensor_scalar(eps1p[:, :], eps_sb[:, :], 1.0, None, ALU.add))
            v.wait_ge(s_w, 64)
            v.wait_ge(s_same, 3)

            def chunks(layer):
                def body(trip):
                    n = layer * PAIRS + trip
                    for b in range(2):
                        at = bass.ds(trip * (2 * C) + b * C, C)
                        v.wait_ge(s_got[b], PER_CHUNK * (n + 1))
                        if not first(layer, trip):
                            v.wait_ge(s_run[b], n)
                        rows = got[b][:, :].rearrange("p (t f) -> p t f", f=D)
                        msg = msgT[b][:, :, :].rearrange("p f t -> p t f")
                        if layer in (0, 3):
                            w = (w0_sb if layer == 0 else w3_sb)[:, at].unsqueeze(2).broadcast_to([P, C, D])
                            nc.vector.tensor_tensor(msg, rows, w, ALU.mult).then_inc(s_used[b], 1)
                        elif layer == 1:
                            v.wait_ge(s_attr[b], 32 * (trip + 1))
                            nc.vector.tensor_tensor(msg, rows, attr[b][:, :].rearrange("p (t f) -> p t f", f=D),
                                                    ALU.add).then_inc(s_used[b], 1)
                            v.wait_ge(s_used[b], n + 1)
                            nc.vector.tensor_scalar(msgT[b][:, :, :], msgT[b][:, :, :], 0.0, None,
                                                    ALU.max).then_inc(s_relu[b], 1)
                        else:
                            nc.vector.tensor_copy(msg, rows).then_inc(s_used[b], 1)
                        nc.vector.tensor_copy(idx[b][:, :], LAYER_ROWS[layer][
                            :, bass.ds(trip * (2 * C) + (2 + b) * C, C)]).then_inc(s_idx[b], 1)
                        v.wait_ge(s_used[b], n + 1)
                        if layer == 1:
                            v.wait_ge(s_relu[b], trip + 1)
                        if b or not first(layer, trip):
                            v.wait_ge(s_scan[1 - b], n + b)
                        nc.vector.scalar_tensor_tensor(
                            msgT[b][:, :, 0], msgT[1 - b][:, :, C - 1], same[:, bass.ds(trip * (2 * C) + b * C, 1)],
                            msgT[b][:, :, 0], ALU.mult, ALU.add).then_inc(s_mixed, 1)
                        v.wait_ge(s_mixed, 2 * n + b + 1)
                        v.wait_ge(s_keep[b], n + 1)
                        flat = msgT[b][:, :, :].rearrange("p f t -> p (f t)")
                        nc.vector.tensor_tensor_scan(flat, keep[b][:, :, :].rearrange("p f t -> p (f t)"), flat,
                                                     0.0, ALU.mult, ALU.add).then_inc(s_scan[b], 1)
                        if layer == 0:
                            hot(PAIRS, trip, b, dst_lo, dst_hi)

                trips(v, layer, body)
                v.wait_ge(s_scan[1], (layer + 1) * PAIRS)
                nc.vector.tensor_copy(tail_sum[:, :], msgT[1][:, :, C - 1]).then_inc(s_tail, 1)

            def degrees():
                v.wait_ge(s_deg, 2)
                link(nc.vector.tensor_copy(deg_in[:, :], hist[1]))
                nc.vector.tensor_scalar(in_clip[:, :], deg_in[:, :], 1.0, None, ALU.max).then_inc(s_clip, 1)
                link(nc.vector.tensor_scalar(has_in[:, :], deg_in[:, :], 1.0, None, ALU.min))
                v.wait_ge(s_clip, 2)
                link(nc.vector.reciprocal(in_inv[:, :], in_clip[:, :]))
                v.wait_ge(s_cum, 1)
                link(nc.vector.tensor_copy(col_tot[:, :], tot_ps))
                link(nc.vector.tensor_tensor_scan(col_cum[:, :], ones[:, 0:COLS], col_tot[:, :], -1.0,
                                                  ALU.mult, ALU.add))
                link(nc.vector.tensor_tensor(col_cum[:, :], col_cum[:, :], col_tot[:, :], ALU.subtract))
                link(nc.vector.tensor_tensor(end_f[:, :], cum_ps, col_cum[:, :], ALU.add))
                link(nc.vector.tensor_scalar(end_f[:, :], end_f[:, :], 0.0, None, ALU.max))
                link(nc.vector.tensor_scalar(end_up[:, :], end_f[:, :], float(E_HALF), float(OVERLAP),
                                             ALU.is_ge, ALU.mult))
                nc.vector.tensor_tensor(end_i[:, :], end_f[:, :], end_up[:, :], ALU.add).then_inc(s_endi, 1)
                v.wait_ge(s_sqrt, 2)
                link(nc.vector.reciprocal(in_scale[:, :], in_sqrt[:, :]))

            def sum_ends(layer, g):
                q = layer * NG + g
                cols = slice(g * G, (g + 1) * G)
                a = agg[q % 2][:, :]
                v.wait_ge(s_end[g], 16 * G * (layer + 1))
                if q >= 2 and layer < 2:
                    v.wait_ge(s_turn, q - 1)
                link(nc.vector.tensor_tensor(cube(a), ends_sum[:, cols, :], over_cols(has_in[:, cols], G), ALU.mult))
                v.wait_ge(s_carry, q + 1)
                if layer == 3:
                    nc.vector.tensor_tensor(a, a, carry_ps(q), ALU.add).then_inc(s_agg, 1)
                    v.wait_ge(s_agg, q + 1)
                    return
                link(nc.vector.tensor_tensor(a, a, carry_ps(q), ALU.add))
                if layer == 1:
                    nc.vector.scalar_tensor_tensor(a, feats[:, cols, :].rearrange("p c f -> p (c f)"), eps1p[:, 0:1],
                                                   a, ALU.mult, ALU.add).then_inc(s_agg, 1)
                else:
                    scale = in_scale if layer == 0 else in_inv
                    nc.vector.tensor_tensor(cube(a), cube(a), over_cols(scale[:, cols], G), ALU.mult)\
                        .then_inc(s_agg, 1)
                v.wait_ge(s_agg, q + 1)

            def finish(layer, g):
                q = layer * NG + g
                cols = slice(g * G, (g + 1) * G)
                f = feats[:, cols, :]
                a = agg[q % 2][:, :]
                if layer < 3:
                    v.wait_ge(s_lin, q + 1)
                    link(nc.vector.tensor_tensor(cube(ta[:, :]), cube(lin_ps(q)),
                                                 bias[layer][:, :].unsqueeze(1).broadcast_to([P, G, D]), ALU.add))
                    if layer == 1:
                        link(nc.vector.tensor_scalar(ta[:, :], ta[:, :], 0.0, None, ALU.max))
                    if layer == 2:
                        link(nc.vector.tensor_tensor(ta[:, :], ta[:, :], a, ALU.add))
                else:
                    link(nc.vector.tensor_scalar(ta[:, :], a, 0.0, None, ALU.max))
                link(nc.vector.tensor_tensor(cube(ta[:, :]), cube(ta[:, :]), f, ALU.add))
                link(nc.vector.tensor_reduce(row_sum[:, :], cube(ta[:, :]), AX.X, ALU.add))
                link(nc.vector.tensor_scalar(row_mean[:, :], row_sum[:, :], 1.0 / D, None, ALU.mult))
                link(nc.vector.tensor_tensor(cube(tb[:, :]), cube(ta[:, :]), over_cols(row_mean[:, :], G),
                                             ALU.subtract))
                link(nc.vector.tensor_tensor(ta[:, :], tb[:, :], tb[:, :], ALU.mult))
                link(nc.vector.tensor_reduce(row_sq[:, :], cube(ta[:, :]), AX.X, ALU.add))
                nc.vector.tensor_scalar(row_var[:, :], row_sq[:, :], 1.0 / D, LN_EPS, ALU.mult, ALU.add)\
                    .then_inc(s_var, 1)
                v.wait_ge(s_std, q + 1)
                link(nc.vector.reciprocal(row_inv[:, :], row_std[:, :]))
                nc.vector.tensor_tensor(f, cube(tb[:, :]), over_cols(row_inv[:, :], G), ALU.mult).then_inc(s_new, 1)
                v.wait_ge(s_new, q + 1)

            def table(layer):
                rel, before = WIDE[layer]
                for c in range(COLS):
                    n = before + c
                    v.wait_ge(s_y, n + 1)
                    if n >= 2:
                        v.wait_ge(s_yst[n % 2], 16 * stored(n, n % 2))
                    nc.vector.tensor_copy(ytile[n % 2][:, rel * D // 2:rel * D],
                                          ps[n % 2][:, rel * D // 2:rel * D]).then_inc(s_yc[1], 1)

            for layer in range(4):
                if layer:
                    stage(layer, 0)
                    stage(layer, 1)
                if layer >= 2:
                    table(layer)
                chunks(layer)
                if layer == 0:
                    degrees()
                for g in range(NG):
                    sum_ends(layer, g)
                    if g:
                        finish(layer, g - 1)
                finish(layer, NG - 1)


_INS = ['x', 'src', 'dst', 'edge_attr_64', 'edge_type_16', 'edge_type_32', 'edge_weight', 'edge_weight1',
        'L0_gnn_W', 'L0_gnn_b', 'L1_gnn_W', 'L1_gnn_b', 'L1_gnn_eps', 'L2_gnn_basis', 'L2_gnn_coeff',
        'L2_gnn_self_weight', 'L2_gnn_bias', 'L3_gnn_weight']
_OUTS = [((3125, 64), 'float32')]


def kernel(**inputs):
    import numpy as _np
    import concourse.bacc as _bacc
    from concourse import mybir as _mybir
    from concourse.bass_utils import run_bass_kernel_spmd as _run

    nc = _bacc.Bacc("TRN2", target_bir_lowering=False, num_devices=1)
    arrays, args = {}, []
    for name in _INS:
        a = _np.ascontiguousarray(inputs[name])
        if a.ndim == 0:
            a = a.reshape(1)
        arrays[f"in_{name}_dram"] = a
        args.append(nc.dram_tensor(f"in_{name}_dram", a.shape, _mybir.dt.from_np(a.dtype), kind="ExternalInput").ap())
    for i, (shape, dtype) in enumerate(_OUTS):
        dt = _mybir.dt.from_np(_np.dtype(dtype))
        args.append(nc.dram_tensor(f"out_{i}_dram", shape, dt, kind="ExternalOutput").ap())
    gnn_stack(nc, *args)
    r = _run(nc, [arrays], core_ids=[0])
    got = tuple(r.results[0][f"out_{i}_dram"] for i in range(len(_OUTS)))
    return got[0]
```

```python
import concourse.bass as bass
from concourse import mybir
from contextlib import ExitStack


def gnn_stack(nc, x, src, dst, edge_attr, etype16, etype32, weight0, weight3,
              W0, b0, W1, b1, eps1, basis, coeff, self_w, b2, W3, out):
    fp32, bf16, i32, fp16 = mybir.dt.float32, mybir.dt.bfloat16, mybir.dt.int32, mybir.dt.float16
    ALU, ACT, AX = mybir.AluOpType, mybir.ActivationFunctionType, mybir.AxisListType

    P = 128
    N, D = x.shape
    E = src.shape[0]
    R2, NB = coeff.shape
    R3 = W3.shape[0]
    HALF = P // 2
    SLOTS = -(-E // P)
    E_HALF = HALF * SLOTS
    HI0 = E - E_HALF
    OVERLAP = E_HALF - HI0
    C = 23
    PAIRS = SLOTS // (2 * C)
    assert PAIRS * 2 * C == SLOTS
    COLS = -(-N // P)
    NPAD = COLS * P
    LASTROWS = N - (COLS - 1) * P
    G = 5
    NG = COLS // G
    GW = G * D
    HC = 2 * COLS
    HCH = COLS
    LN_EPS = 1e-5
    BANK = 512
    KF = BANK // C
    PICKS = 6
    NPP = PICKS // 2
    CENTER = NPAD // 2
    HOTS = 3
    PICKED_CHUNKS = 2 * PAIRS - 2
    PARAMS = 16 * 12
    INITS = 8
    INEXACT = dict(allow_small_or_imprecise_dtypes=True)

    Y = 3

    def stored(n, y):
        return (n + Y - 1 - y) // Y

    def whole(layer, trip, b):
        return layer > 1 or (isinstance(trip, int) and (trip, b) in ((0, 0), (PAIRS - 1, 1)))

    def rows_in(layer, trip, b):
        before = sum(C * PAIRS - (PICKS * (PAIRS - 1) if l < 2 else 0) for l in range(layer))
        if layer < 2:
            extra = PICKS if b == 0 or whole(layer, trip, b) else 0
            rows = (C - PICKS) * trip + (C - PICKS + extra + before)
        else:
            rows = C * trip + (C + before)
        return 16 * rows

    assert NG * G == COLS and COLS == 25 and PICKS % 2 == 0 and PICKS % HOTS == 0 and PICKS > HOTS and CENTER <= 2048

    def dram(name, shape):
        return nc.dram_tensor(name, shape, fp32, kind="Internal").ap()

    table0 = dram("table0", [NPAD, D])
    table1 = dram("table1", [NPAD, D])
    table2 = dram("table2", [NPAD * R2, D])
    table3 = dram("table3", [NPAD * R3, D])
    sums = dram("running_sums", [P * SLOTS + 1, D])
    tables = [table0, table1, table2, table3]
    sums_pt = sums[0:P * SLOTS, :].rearrange("(p t) f -> p (t f)", t=SLOTS)

    def by_col(table):
        return table.rearrange("(c p) f -> p c f", p=P)

    def halves(vec):
        return (vec[0:E_HALF].rearrange("(p t) -> p t", t=SLOTS),
                vec[HI0:E].rearrange("(p t) -> p t", t=SLOTS))

    attr_lo = edge_attr[0:E_HALF, :].rearrange("(p t) f -> p (t f)", t=SLOTS)
    attr_hi = edge_attr[HI0:E, :].rearrange("(p t) f -> p (t f)", t=SLOTS)

    ctx = ExitStack()
    with ctx:
        def sb(name, shape, dt=fp32):
            return ctx.enter_context(nc.sbuf_tensor(name, shape, dt))

        def sem(name):
            return ctx.enter_context(nc.semaphore(name))

        src_i = sb("src_i", [P, SLOTS + 2 * C], i32)
        dst_i = sb("dst_i", [P, SLOTS], i32)
        rows2 = sb("rows2", [P, SLOTS + 2 * C], i32)
        rows3 = sb("rows3", [P, SLOTS + 2 * C], i32)
        key_i = sb("key_i", [P, SLOTS], i32)
        src_lo, src_hi, dst_lo, dst_hi = (sb(n, [P, SLOTS], bf16) for n in ("src_lo", "src_hi", "dst_lo", "dst_hi"))
        edge_w = sb("edge_w", [P, SLOTS])
        same = sb("same", [P, SLOTS])
        idx = [sb(f"idx{b}", [P, C], i32) for b in range(2)]
        got = [sb(f"got{b}", [P, C * D]) for b in range(2)]
        attr = [sb(f"attr{b}", [P, C * D]) for b in range(2)]
        msgT = [sb(f"msgT{b}", [P, D, C]) for b in range(2)]
        run = [sb(f"run{b}", [P, C * D]) for b in range(2)]
        hot_lo = [sb(f"hot_lo{b}", [P, HALF, C], bf16) for b in range(2)]
        hot_hi = [sb(f"hot_hi{b}", [P, HC, C], bf16) for b in range(2)]
        src_c = sb("src_c", [P, SLOTS], fp16)
        ident_h = sb("ident_h", [P, P], fp16)
        ramp_f = sb("ramp_f", [P, P])
        ramp_lo = sb("ramp_lo", [P, HALF, C], bf16)
        ramp_hi = sb("ramp_hi", [P, HC, C], bf16)
        part_f = sb("part_f", [P, 1])
        ident = sb("ident", [P, P])
        ident_b = sb("ident_b", [P, P], bf16)
        upper = sb("upper", [P, P])
        ones = sb("ones", [P, P])
        zero_b = sb("zero_b", [P, HALF], bf16)
        feats = sb("feats", [P, COLS, D])
        side = sb("side", [P, COLS, D])
        aggT = sb("aggT", [D, G * P])
        part_hm = sb("part_hm", [P, G, 2 * D], bf16)
        part_hl = sb("part_hl", [P, G, 2 * D], bf16)
        parts = sb("parts", [P, 2 * NPAD], bf16)
        hmT, hlT = parts[:, 0:NPAD], parts[:, NPAD:2 * NPAD]
        table_parts = parts[:, 0:COLS * 3 * D].rearrange("p (c f) -> p c f", f=3 * D)
        ends_sum = sb("ends_sum", [P, COLS, D])
        zero_row = sb("zero_row", [1, D])
        resid = sb("resid", [P, COLS, D])
        tail_sum = sb("tail_sum", [P, D])
        carry_hot = sb("carry_hot", [P, NPAD])
        next_i = sb("next_i", [P, 1], i32)
        last_dst, goes_on, eps_sb, eps1p = (sb(n, [P, 1]) for n in ("last_dst", "goes_on", "eps_sb", "eps1p"))
        (deg_out, out_sqrt, out_scale, deg_in, has_in, in_clip, in_sqrt, in_scale, in_inv, col_tot, col_cum,
         end_f, end_up) = (sb(n, [P, COLS]) for n in (
             "deg_out", "out_sqrt", "out_scale", "deg_in", "has_in", "in_clip", "in_sqrt", "in_scale",
             "in_inv", "col_tot", "col_cum", "end_f", "end_up"))
        deg64 = sb("deg64", [HALF, HC])
        end_i = sb("end_i", [P, COLS], i32)
        ta = sb("ta", [P, GW])
        tb = sb("tb", [P, GW])
        agg = [sb(f"agg{b}", [P, GW]) for b in range(2)]
        row_sum, row_mean, row_sq, row_var, row_std, row_inv = (
            sb(n, [P, G]) for n in ("row_sum", "row_mean", "row_sq", "row_var", "row_std", "row_inv"))
        w_raw = sb("w_raw", [D, 2, D])
        wT = sb("wT", [D, 2, D])
        sw_sb = sb("sw_sb", [P, D])
        rel3_sb = sb("rel3_sb", [P, R3 * D])
        bias = [sb(f"bias{l}", [P, D]) for l in range(3)]
        coeff_sb = sb("coeff_sb", [R2, NB])
        coeffT = sb("coeffT", [NB, R2])
        rel2, rel3, self3 = ([sb(f"{n}_{part}", [P, w], bf16) for part in ("h", "m", "x")]
                             for n, w in (("rel2", R2 * D), ("rel3", R3 * D), ("self", D)))
        ytiles = sb("ytiles", [P, Y, R2 * D])
        basis_sb = ytiles[0:NB, 0:2, :].rearrange("b a n -> b (a n)")
        rel2_sb = ytiles[:, 2, :]

        def in_ytile(y, dt):
            return ytiles[:, y, 0:COLS * P // 2].bitcast(dt).rearrange("p (c e) -> p c e", e=P)

        hot_src = [in_ytile(0, bf16), in_ytile(1, bf16),
                   ends_sum[:, :, :].rearrange("p c f -> p (c f)").bitcast(bf16).rearrange("p (c e) -> p c e", e=P)]
        ramp_src = in_ytile(2, fp16)

        psA = ctx.enter_context(nc.psum_tensor("psA", [P, 4 * BANK], fp32))
        psB = ctx.enter_context(nc.psum_tensor("psB", [P, 4 * BANK], fp32))
        keep = psB[:, 0:KF * C].rearrange("p (f t) -> p f t", t=C)
        weights = psA[:, 0:SLOTS]
        attr_ps = psA[:, 0:C * D]
        node_rows = psB[:, BANK:BANK + PICKS * P // 2].bitcast(fp16).rearrange("p (s e) -> p s e", e=P)

        def picked(at):
            return psB[:, (2 + at % 2) * BANK:(2 + at % 2) * BANK + 6 * D].rearrange("p (s k f) -> p s k f", s=2, k=3)

        hist = psA[0:HALF, 3 * BANK:3 * BANK + HC]
        deg_ps = psA[:, 2 * BANK + 2 * D:2 * BANK + 2 * D + HCH]
        cum_ps = psA[:, 2 * BANK:2 * BANK + COLS]
        tot_ps = psA[:, 2 * BANK + D:2 * BANK + D + COLS]
        carry_ps = psB[:, 0:COLS * D]
        turn_ps = psA[0:D, 2 * BANK:2 * BANK + G * P]
        turn_parts = psA[:, 2 * BANK:2 * BANK + G * P].bitcast(bf16).rearrange("p (k n) -> p k n", k=2)

        def lin_ps(q):
            return psA[:, (q % 2) * BANK:(q % 2) * BANK + GW]

        def y_ps(h):
            return psB[:, (h % 2) * 2 * BANK:(h % 2 + 1) * 2 * BANK]

        def over_cols(v, n):
            return v.unsqueeze(2).broadcast_to([P, n, D])

        def cube(t):
            return t.rearrange("p (c f) -> p c f", f=D)

        s_init = sem("buffers_cleared")
        s_src, s_dst, s_typ, s_w, s_x, s_par = (
            sem(n) for n in ("src_loaded", "dst_loaded", "types_loaded", "weights_loaded", "x_loaded",
                             "params_loaded"))
        s_pool = sem("ramps_made")
        s_v = sem("vector_steps")
        s_const = sem("consts_ready")
        s_same = sem("segment_flags_ready")
        s_hot = [sem(f"hot_made{b}") for b in range(2)]
        s_cnt = [sem(f"hot_counted{b}") for b in range(2)]
        s_cnt64 = sem("degrees_counted")
        s_deg64 = sem("degrees_copied")
        s_deg = sem("degrees_spread")
        s_clip = sem("degrees_clipped")
        s_sqrt = sem("degree_sqrt_done")
        s_cum = sem("columns_summed")
        s_table = sem("table_stored")
        s_scaled = sem("scaled_ready")
        s_idx = [sem(f"idx_staged{b}") for b in range(2)]
        s_got = [sem(f"rows_gathered{b}") for b in range(2)]
        s_used = [sem(f"rows_used{b}") for b in range(2)]
        s_attr = [sem(f"attr_loaded{b}") for b in range(2)]
        s_mixed = sem("chunk_carried")
        s_keep = sem("keep_spread")
        s_resid = sem("residual_ready")
        s_zero = sem("keep_zeroed")
        s_wps = sem("weights_in_psum")
        s_aps = sem("attr_in_psum")
        s_relc = sem("relations_copied")
        s_rel2 = sem("relations_doubled")
        s_pv = sem("pool_steps")
        s_tparts = sem("table_parts_ready")
        s_rep = sem("nodes_replicated")
        s_sel = sem("source_hots_made")
        s_mul = sem("slots_picked")
        s_filled = sem("picks_placed")
        s_moved = [sem(f"rows_turned{b}") for b in range(2)]
        s_scan = [sem(f"chunk_scanned{b}") for b in range(2)]
        s_run = [sem(f"sums_copied{b}") for b in range(2)]
        s_wr = [sem(f"sums_stored{b}") for b in range(2)]
        s_zrow = sem("zero_row_stored")
        s_endi = sem("end_rows_ready")
        s_end = [sem(f"ends_gathered{g}") for g in range(NG)]
        s_tail = sem("tail_ready")
        s_carry = sem("carry_multiplied")
        s_agg = sem("agg_ready")
        s_turn = sem("agg_transposed")
        s_aggT = sem("aggT_copied")
        s_lin = sem("linear_done")
        s_new = sem("features_ready")
        s_var = sem("variance_ready")
        s_std = sem("std_ready")
        s_csum = sem("carry_copied")
        s_parts = sem("parts_ready")
        s_xt = sem("parts_transposed")
        s_xT = sem("parts_copied")
        s_wparts = sem("weight_parts_ready")
        s_wt = sem("weights_multiplied")
        s_wc = sem("weights_copied")
        s_y = sem("table_product")
        s_yc = sem("table_copied")
        s_yst = [sem(f"wide_table_stored{y}") for y in range(Y)]
        s_out = sem("output_stored")
        s_go = sem("chunk_started")

        LAYER_ROWS = [src_i, src_i, rows2, rows3]
        WIDE = {2: (R2, 0), 3: (R3, COLS)}

        def halves_before(layer, c):
            return 2 * c if layer == 2 else 2 * COLS + c

        def trips(eng, layer, body):
            if layer < 2:
                body(0)
                with eng.Fori(1, PAIRS - 2) as trip:
                    body(trip)
                body(PAIRS - 2)
                body(PAIRS - 1)
            else:
                with eng.Fori(0, PAIRS) as trip:
                    body(trip)

        def first(layer, trip):
            return layer == 0 and isinstance(trip, int) and trip == 0

        def following(layer, trip, b):
            if layer > 1 or (isinstance(trip, int) and trip == PAIRS - 1):
                return None
            return (trip, 1) if b == 0 else (trip + 1, 0)

        def pick_number(layer, trip, b):
            return 2 * trip + (layer * PICKED_CHUNKS + b - 1)

        def pair_number(b, j):
            return NPP * (b + 1) + j

        block = ctx.enter_context(nc.Block())

        @block.sync
        def _(sp):
            sp.wait_ge(s_init, INITS)
            for n, h in enumerate(halves(src)):
                sp.dma_start(src_i[n * HALF:(n + 1) * HALF, 0:SLOTS], h).then_inc(s_src, 16)
            sp.dma_start(feats[:, 0:COLS - 1, :], by_col(x[0:(COLS - 1) * P, :])).then_inc(s_x, 16)
            sp.dma_start(feats[0:LASTROWS, COLS - 1, :], x[(COLS - 1) * P:N, :]).then_inc(s_x, 16)
            for n, h in enumerate(halves(dst)):
                sp.dma_start(dst_i[n * HALF:(n + 1) * HALF, :], h).then_inc(s_dst, 16)
            after = dst[SLOTS:SLOTS + E_HALF].rearrange("(p t) -> p t", t=SLOTS)
            sp.dma_start(next_i[0:HALF, :], after[:, 0:1], allow_slow_non_contiguous=True).then_inc(s_dst, 16)
            after = dst[HI0 + SLOTS:E].rearrange("(p t) -> p t", t=SLOTS)
            sp.dma_start(next_i[HALF:P - 1, :], after[:, 0:1], allow_slow_non_contiguous=True).then_inc(s_dst, 16)

            def load_weights(v):
                for n, h in enumerate(halves(v)):
                    sp.dma_start(edge_w[n * HALF:(n + 1) * HALF, :], h).then_inc(s_w, 16)

            load_weights(weight0)
            for v, t in ((etype32, rows2), (etype16, rows3)):
                for n, h in enumerate(halves(v)):
                    sp.dma_start(t[n * HALF:(n + 1) * HALF, 0:SLOTS], h).then_inc(s_typ, 16)

            sp.dma_start(sums[P * SLOTS:P * SLOTS + 1, :], zero_row[:, :]).then_inc(s_zrow, 16)

            def store_sums(layer):
                def load_attr(b, at):
                    for n, half in enumerate((attr_lo, attr_hi)):
                        sp.dma_start(attr[b][n * HALF:(n + 1) * HALF, :],
                                     half[:, bass.ds(at, C * D)]).then_inc(s_attr[b], 16)

                def body(trip, last=False):
                    for b in range(2):
                        sp.wait_ge(s_run[b], layer * PAIRS + 1 + trip)
                        sp.dma_start(sums_pt[:, bass.ds(trip * (2 * C * D) + b * C * D, C * D)],
                                     run[b][:, :]).then_inc(s_wr[b], 16)
                        if layer == 1 and not last:
                            load_attr(b, trip * (2 * C * D) + (2 + b) * C * D)

                if layer == 1:
                    for b in range(2):
                        load_attr(b, b * C * D)
                with sp.Fori(0, PAIRS - 1) as trip:
                    body(trip)
                body(PAIRS - 1, last=True)

            def store_table(layer):
                if layer < 2:
                    for g in range(NG):
                        sp.wait_ge(*((s_scaled, g + 1) if layer == 0 else (s_new, g + 1)))
                        t = side if layer == 0 else feats
                        sp.dma_start(by_col(tables[layer])[:, g * G:(g + 1) * G, :],
                                     t[:, g * G:(g + 1) * G, :]).then_inc(s_table, 16)
                    return
                rel, before = WIDE[layer]
                wide = tables[layer].rearrange("(n r) f -> n (r f)", r=rel)
                for c in range(COLS):
                    sp.wait_ge(s_yc, halves_before(layer, c + 1))
                    y = (before + c) % Y
                    sp.dma_start(wide[c * P:(c + 1) * P, :], ytiles[:, y, 0:rel * D]).then_inc(s_yst[y], 16)

            for layer in range(4):
                store_table(layer)
                if layer == 0:
                    sp.wait_ge(s_wps, 1)
                    load_weights(weight3.rearrange("e o -> (e o)"))
                store_sums(layer)
            sp.wait_ge(s_new, 4 * NG)
            sp.dma_start(by_col(out[0:(COLS - 1) * P, :]), feats[:, 0:COLS - 1, :]).then_inc(s_out, 16)
            sp.dma_start(out[(COLS - 1) * P:N, :], feats[0:LASTROWS, COLS - 1, :]).then_inc(s_out, 16)
            sp.wait_ge(s_out, 32)

        @block.gpsimd
        def _(pool):
            made = [
                nc.gpsimd.iota(ramp_f[:, :], pattern=[[1, P]], base=0, channel_multiplier=0, **INEXACT),
                nc.gpsimd.iota(part_f[:, :], pattern=[[0, 1]], base=0, channel_multiplier=1, **INEXACT),
                nc.gpsimd.iota(ramp_lo[:, :, :], pattern=[[1, HALF], [0, C]], base=0, channel_multiplier=0, **INEXACT),
                nc.gpsimd.iota(ramp_hi[:, :, :], pattern=[[1, 2], [2, HCH], [0, C]], base=0, channel_multiplier=0,
                               **INEXACT),
                nc.gpsimd.iota(carry_hot[:, :], pattern=[[1, NPAD]], base=0, channel_multiplier=0, **INEXACT),
                nc.gpsimd.memset(ones[:, :], 1.0),
            ]
            for ins in made:
                ins.then_inc(s_pool, 1)

            steps = [0]

            def link(ins):
                steps[0] += 1
                ins.then_inc(s_pv, 1)
                pool.wait_ge(s_pv, steps[0])

            def weight_parts(w, value):
                cols = value.shape[1]
                low, high = slice(0, D), slice(D, P)
                rest = run[0]
                for at in range(0, cols, 2 * BANK):
                    n = min(2 * BANK, cols)
                    h, m, x = [t[:, at:at + n] for t in w]
                    link(nc.gpsimd.tensor_copy(h, value[:, at:at + n]))
                    link(nc.gpsimd.tensor_tensor(rest[:, 0:n], value[:, at:at + n], h, ALU.subtract))
                    link(nc.gpsimd.tensor_copy(m, rest[:, 0:n]))
                    link(nc.gpsimd.tensor_tensor(x[low], rest[low, 0:n], m[low], ALU.subtract))
                    link(nc.gpsimd.tensor_copy(x[high], h[high]))

            pool.wait_ge(s_par, PARAMS)
            weight_parts(self3, sw_sb[:, :])
            weight_parts(rel3, rel3_sb[:, :])
            pool.wait_ge(s_rel2, 16)
            weight_parts(rel2, rel2_sb)
            pool.sem_inc(s_wparts, 1)
            nc.gpsimd.iota(ramp_src, pattern=[[P, COLS], [0, P]], base=-CENTER, channel_multiplier=1,
                           **INEXACT).then_inc(s_pool, 1)

            def gather_edges(layer):
                if layer < 2:
                    pool.wait_ge(s_table, 16 * NG * (layer + 1))
                else:
                    for y in range(Y):
                        pool.wait_ge(s_yst[y], 16 * stored(WIDE[layer][1] + COLS, y))

                def body(trip):
                    for b in range(2):
                        pool.wait_ge(s_idx[b], layer * (PAIRS + 1) + 1 + trip)
                        if not first(layer, trip):
                            pool.wait_ge(s_used[b], layer * PAIRS + trip)
                        pool.sem_inc(s_go, 1)
                        for s in range(C if whole(layer, trip, b) else C - PICKS):
                            nc.gpsimd.indirect_dma_start(
                                out=got[b][:, s * D:(s + 1) * D], out_offset=None, in_=tables[layer],
                                in_offset=bass.IndirectOffsetOnAxis(ap=idx[b][:, s:s + 1], axis=0),
                            ).then_inc(s_got[b], 16)

                trips(pool, layer, body)

            def gather_ends(layer):
                for b in range(2):
                    pool.wait_ge(s_wr[b], 16 * PAIRS * (layer + 1))
                pool.wait_ge(s_endi, 1)
                pool.wait_ge(s_zrow, 16)
                if layer:
                    pool.wait_ge(s_agg, NG * layer)
                for c in range(COLS):
                    nc.gpsimd.indirect_dma_start(
                        out=ends_sum[:, c, :], out_offset=None, in_=sums,
                        in_offset=bass.IndirectOffsetOnAxis(ap=end_i[:, c:c + 1], axis=0),
                    ).then_inc(s_end[c // G], 16)

            for layer in range(4):
                gather_edges(layer)
                gather_ends(layer)

        @block.scalar
        def _(act):
            act.wait_ge(s_init, INITS)
            act.dma_start(w_raw[:, 0, :], W0).then_inc(s_par, 16)
            act.dma_start(w_raw[:, 1, :], W1).then_inc(s_par, 16)
            for t, v in zip(bias, (b0, b1, b2)):
                act.dma_start(t[:, :], v.unsqueeze(0).broadcast_to([P, D])).then_inc(s_par, 16)
            act.dma_start(eps_sb[:, :], eps1.unsqueeze(0).broadcast_to([P, 1])).then_inc(s_par, 16)
            act.dma_start(coeff_sb[:, :], coeff).then_inc(s_par, 16)
            act.dma_start(basis_sb, basis.rearrange("b i o -> b (i o)")).then_inc(s_par, 16)
            for h in range(2):
                half = slice(h * D, (h + 1) * D)
                act.dma_start(sw_sb[half, :], self_w).then_inc(s_par, 16)
                act.dma_start(rel3_sb[half, :].rearrange("i (r o) -> i r o", r=R3),
                              W3.rearrange("r i o -> i r o")).then_inc(s_par, 16)
            act.wait_ge(s_wt, 1)
            nc.scalar.copy(wT[:, :, :], psA[0:D, 0:2 * D].rearrange("i (l o) -> i l o", l=2)).then_inc(s_wc, 1)
            nc.scalar.copy(coeffT[:, :], psA[0:NB, BANK:BANK + R2]).then_inc(s_wc, 1)
            act.wait_ge(s_wt, 2)
            nc.scalar.copy(rel2_sb[0:D, :].rearrange("i (r o) -> i o r", r=R2),
                           psB[0:D, :].rearrange("i (o r) -> i o r", r=R2)).then_inc(s_relc, 1)
            act.wait_ge(s_relc, 1)
            act.dma_start(rel2_sb[D:P, :], rel2_sb[0:D, :]).then_inc(s_rel2, 16)
            act.wait_ge(s_clip, 1)
            nc.scalar.activation(out_sqrt[:, :], deg_out[:, :], ACT.Sqrt).then_inc(s_sqrt, 1)
            act.wait_ge(s_same, 3)

            def spread(layer, trip, b):
                if b or not first(layer, trip):
                    act.wait_ge(s_scan[1 - b], layer * PAIRS + trip + b)
                nc.scalar.copy(keep[:, :, 1:C],
                               same[:, bass.ds(trip * (2 * C) + b * C + 1, C - 1)]
                               .unsqueeze(1).broadcast_to([P, KF, C - 1])).then_inc(s_keep, 1)

            def chunks(layer):
                act.wait_ge(s_zero, layer + 1)
                if layer in (0, 3):
                    act.wait_ge(s_w, 32 if layer == 0 else 64)
                    if layer == 0:
                        act.wait_ge(s_wc, 2)
                    nc.scalar.copy(weights, edge_w[:, :]).then_inc(s_wps, 1)

                def stage_attr(trip, b):
                    act.wait_ge(s_attr[b], 32 * (trip + 1))
                    act.wait_ge(s_used[1 - b], layer * PAIRS + trip + b)
                    nc.scalar.copy(attr_ps, attr[b][:, :]).then_inc(s_aps, 1)

                def body(trip):
                    n = layer * PAIRS + trip
                    for b in range(2):
                        next_chunk = (trip, 1) if b == 0 else (trip + 1, 0)
                        if b and isinstance(trip, int) and trip == PAIRS - 1:
                            next_chunk = None
                        if layer == 1:
                            if isinstance(trip, int) and trip == 0 and b == 0:
                                stage_attr(trip, b)
                                spread(layer, trip, b)
                            act.wait_ge(s_used[b], n + 1)
                            nc.scalar.activation(msgT[b][:, :, :], msgT[b][:, :, :], ACT.Relu)\
                                .then_inc(s_moved[b], 1)
                            if next_chunk:
                                stage_attr(*next_chunk)
                        elif layer == 2:
                            spread(layer, trip, b)
                            act.wait_ge(s_got[b], rows_in(layer, trip, b))
                            nc.scalar.copy(msgT[b][:, :, :].rearrange("p f t -> p t f"),
                                           got[b][:, :].rearrange("p (t f) -> p t f", f=D)).then_inc(s_used[b], 1)
                        else:
                            spread(layer, trip, b)
                        act.wait_ge(s_scan[b], n + 1)
                        if not first(layer, trip):
                            act.wait_ge(s_wr[b], n * 16)
                        nc.scalar.copy(run[b][:, :].rearrange("p (t f) -> p f t", f=D),
                                       msgT[b][:, :, :]).then_inc(s_run[b], 1)
                        if layer == 1 and next_chunk:
                            spread(layer, *next_chunk)

                trips(act, layer, body)

            def nodes(layer):
                if layer == 0:
                    act.wait_ge(s_clip, 2)
                    nc.scalar.activation(in_sqrt[:, :], in_clip[:, :], ACT.Sqrt).then_inc(s_sqrt, 1)
                act.wait_ge(s_carry, layer + 1)
                if layer:
                    act.wait_ge(s_agg, NG * layer)
                else:
                    act.wait_ge(s_table, 16 * NG)
                if layer != 1:
                    nc.scalar.copy(side[:, :, :].rearrange("p c f -> p (c f)"), carry_ps).then_inc(s_csum, 1)

                def turned(g):
                    q = layer * NG + g
                    act.wait_ge(s_xt, q - NG + 1)
                    for k, t in enumerate((hmT, hlT)):
                        nc.scalar.copy(t[:, g * G * P:(g + 1) * G * P], turn_parts[:, k, :]).then_inc(s_xT, 1)

                def table(c):
                    rel, before = WIDE[layer + 1]
                    n = before + c
                    if n >= Y:
                        act.wait_ge(s_yst[n % Y], 16 * stored(n, n % Y))
                    for h in range(rel * D // (2 * BANK)):
                        y = halves_before(layer + 1, c) + h
                        act.wait_ge(s_y, y + 1)
                        nc.scalar.copy(ytiles[:, n % Y, h * 2 * BANK:(h + 1) * 2 * BANK], y_ps(y))\
                            .then_inc(s_yc, 1)

                def copy_aggT(g):
                    if layer < 2 and g < NG:
                        q = layer * NG + g
                        act.wait_ge(s_turn, q + 1)
                        if q:
                            act.wait_ge(s_lin, q)
                        nc.scalar.copy(aggT[:, :], turn_ps).then_inc(s_aggT, 1)

                def root(g):
                    if g < NG:
                        act.wait_ge(s_var, layer * NG + g + 1)
                        nc.scalar.activation(row_std[:, :], row_var[:, :], ACT.Sqrt).then_inc(s_std, 1)

                if layer in (0, 3):
                    for g in range(NG):
                        copy_aggT(g)
                        root(g)
                else:
                    copy_aggT(0)
                    copy_aggT(1)
                    root(0)
                    turned(0)
                    for g in range(NG):
                        c = g * G
                        table(c)
                        root(g + 1)
                        copy_aggT(g + 2)
                        table(c + 1)
                        table(c + 2)
                        if g + 1 < NG:
                            turned(g + 1)
                        table(c + 3)
                        table(c + 4)

            for layer in range(4):
                chunks(layer)
                nodes(layer)

        @block.tensor
        def _(pe):
            def count(base, trip, b):
                pe.wait_ge(s_hot[b], 2 * (base + trip) + 2)
                for s in range(C):
                    last = nc.tensor.matmul(hist, hot_lo[b][:, :, s], hot_hi[b][:, :, s],
                                            start=False, stop=False, skip_group_check=True)
                last.then_inc(s_cnt[b], 1)

            def count_sources(lo, hi):
                with pe.Fori(lo, hi) as trip:
                    for b in range(2):
                        count(0, trip, b)

            def pick(layer, trip, b):
                n = pick_number(layer, trip, b)
                start = isinstance(n, int) and n == 0

                def replicate(trip, b):
                    for i in range(PICKS):
                        slot = bass.ds(trip * (2 * C) + (b + 1) * C - PICKS + i, 1)
                        last = nc.tensor.transpose(node_rows[:, i, :], src_c[:, slot].broadcast_to([P, P]),
                                                   ident_h[:, :])
                    last.then_inc(s_rep, 1)

                if isinstance(trip, int) and trip == 0:
                    if not start:
                        pe.wait_ge(s_sel, PICKS * n)
                    replicate(trip, b)
                for j in range(NPP):
                    if j >= 2 or not start:
                        pe.wait_ge(s_filled, NPP * n + j - 1)
                    for s in range(2):
                        i = 2 * j + s
                        if i == PICKS - 2 and following(layer, trip, b):
                            pe.wait_ge(s_sel, PICKS * (n + 1))
                            replicate(*following(layer, trip, b))
                        pe.wait_ge(s_sel, PICKS * n + i + 1)
                        for c in range(COLS):
                            last = nc.tensor.matmul(
                                picked(pair_number(b, j))[:, s, :, :].rearrange("p k f -> p (k f)"),
                                hot_src[i % HOTS][:, c, :], table_parts[:, c, :], start=(c == 0), stop=(c == COLS - 1))
                        last.then_inc(s_mul, 1)

            def bound(start):
                last = nc.tensor.matmul(hist, zero_b[:, :], zero_b[:, 0:HC], start=start, stop=not start,
                                        skip_group_check=True)
                if not start:
                    last.then_inc(s_cnt64, 1)

            def spread_degrees(n):
                pe.wait_ge(s_deg64, n)
                for h in range(2):
                    last = nc.tensor.matmul(deg_ps[h * HALF:(h + 1) * HALF, :], ident[0:HALF, 0:HALF],
                                            deg64[:, h * HCH:(h + 1) * HCH], start=True, stop=True)
                last.then_inc(s_deg, 1)

            pe.wait_ge(s_init, INITS)
            bound(True)
            count_sources(0, 2)
            pe.wait_ge(s_const, 1)
            pe.wait_ge(s_par, PARAMS)
            for l in range(2):
                nc.tensor.transpose(psA[0:D, l * D:(l + 1) * D], w_raw[:, l, :], ident[0:D, 0:D])
            nc.tensor.transpose(psA[0:NB, BANK:BANK + R2], coeff_sb[:, :], ident[0:R2, 0:R2]).then_inc(s_wt, 1)
            PARTS = 4
            for part in range(PARTS):
                count_sources(part + 2, part + 3)
                pe.wait_ge(s_wc, 2)
                for o in range(part * D // PARTS, (part + 1) * D // PARTS):
                    last = nc.tensor.matmul(psB[0:D, o * R2:(o + 1) * R2], basis_sb[:, o:D * D:D], coeffT[:, :],
                                            start=True, stop=True)
            last.then_inc(s_wt, 1)
            count_sources(PARTS + 2, PAIRS)
            bound(False)
            spread_degrees(1)
            bound(True)
            pe.wait_ge(s_tparts, 1)
            pe.wait_ge(s_relc, 1)

            def beside_chunks(trip):
                for b in range(2):
                    if following(0, trip, b):
                        pick(0, *following(0, trip, b))
                    count(PAIRS, trip, b)

            trips(pe, 0, beside_chunks)
            bound(False)
            spread_degrees(2)
            pe.wait_ge(s_clip, 2)
            nc.tensor.matmul(cum_ps, upper[:, :], deg_in[:, :], start=True, stop=True)
            nc.tensor.matmul(tot_ps, ones[:, :], deg_in[:, :], start=True, stop=True).then_inc(s_cum, 1)

            def picks(trip):
                for b in range(2):
                    if following(1, trip, b):
                        pick(1, *following(1, trip, b))

            def by_parts(out_ps, c, w, cols):
                at = slice(c * P, (c + 1) * P)
                for n, (x_part, w_part) in enumerate(((hmT, w[0]), (hmT, w[1]), (hlT, w[2]))):
                    last = nc.tensor.matmul(out_ps, x_part[:, at], w_part[:, cols], start=(n == 0), stop=(n == 2))
                return last

            def nodes(layer):
                pe.wait_ge(s_tail, layer + 1)
                for c in range(COLS):
                    last = nc.tensor.matmul(carry_ps[:, c * D:(c + 1) * D], carry_hot[:, c * P:(c + 1) * P],
                                            tail_sum[:, :], start=True, stop=True)
                last.then_inc(s_carry, 1)

                def turn_sums(g):
                    if layer > 1 or g >= NG:
                        return
                    q = layer * NG + g
                    pe.wait_ge(s_agg, q + 1)
                    if q:
                        pe.wait_ge(s_aggT, q)
                    if layer == 1 and g >= 2:
                        pe.wait_ge(s_xT, 2 * (q - NG - 1))
                    for j in range(G):
                        last = nc.tensor.transpose(turn_ps[:, j * P:(j + 1) * P],
                                                   cube(agg[q % 2][:, :])[:, j, :], ident[:, :])
                    last.then_inc(s_turn, 1)

                def linear(g):
                    if layer > 2 or g >= NG:
                        return
                    q = layer * NG + g
                    if layer < 2:
                        pe.wait_ge(s_aggT, q + 1)
                    if q >= 2:
                        pe.wait_ge(s_new, q - 1)
                    for j in range(G):
                        out_ps = lin_ps(q)[:, j * D:(j + 1) * D]
                        if layer < 2:
                            last = nc.tensor.matmul(out_ps, aggT[:, j * P:(j + 1) * P], wT[:, layer, :],
                                                    start=True, stop=True)
                        else:
                            last = by_parts(out_ps, g * G + j, self3, slice(0, D))
                    last.then_inc(s_lin, 1)

                def turn_parts_of(g):
                    q = layer * NG + g
                    pe.wait_ge(s_parts, q - NG + 1)
                    if q > NG:
                        pe.wait_ge(s_xT, 2 * (q - NG))
                    if layer < 2:
                        pe.wait_ge(s_aggT, min(q + 2, NG * (layer + 1)))
                    for k, t in enumerate((part_hm, part_hl)):
                        for j in range(G):
                            last = nc.tensor.transpose(turn_parts[:, k, j * P:(j + 1) * P], t[:, j, :],
                                                       ident_b[:, :])
                    last.then_inc(s_xt, 1)

                def table(c):
                    pe.wait_ge(s_xT, 2 * (layer * NG + c // G - NG + 1))
                    rel, _ = WIDE[layer + 1]
                    w = rel2 if layer == 1 else rel3
                    for h in range(rel * D // (2 * BANK)):
                        y = halves_before(layer + 1, c) + h
                        if y >= 2:
                            pe.wait_ge(s_yc, y - 1)
                        for k in range(2):
                            col = (2 * h + k) * BANK
                            last = by_parts(y_ps(y)[:, k * BANK:(k + 1) * BANK], c, w, slice(col, col + BANK))
                        last.then_inc(s_y, 1)

                if layer in (0, 3):
                    for g in range(NG):
                        turn_sums(g)
                        linear(g)
                    return
                turn_sums(0)
                linear(0)
                turn_sums(1)
                linear(1)
                turn_parts_of(0)
                pe.wait_ge(s_csum, layer + 1)
                pe.wait_ge(s_wparts, 1)
                for g in range(NG):
                    c = g * G
                    table(c)
                    turn_sums(g + 2)
                    table(c + 1)
                    linear(g + 2)
                    table(c + 2)
                    if g + 1 < NG:
                        turn_parts_of(g + 1)
                    table(c + 3)
                    table(c + 4)

            for layer in range(4):
                if layer == 1:
                    pe.wait_ge(s_tparts, 2)
                    trips(pe, 1, picks)
                nodes(layer)

        @block.vector
        def _(v):
            steps = [0]

            def link(ins):
                steps[0] += 1
                ins.then_inc(s_v, 1)
                v.wait_ge(s_v, steps[0])

            for t, value in ((src_i[:, SLOTS:], 0), (rows2[:, SLOTS:], 0), (rows3[:, SLOTS:], 0),
                             (feats[:, COLS - 1, :], 0.0), (next_i[:, :], -1), (zero_b[:, :], 0.0),
                             (msgT[1][:, :, C - 1], 0.0), (zero_row[:, :], 0.0)):
                nc.vector.memset(t, value).then_inc(s_init, 1)

            def split(nodes, lo, hi):
                link(nc.vector.tensor_scalar(key_i[:, :], nodes, HALF - 1, None, ALU.bitwise_and))
                link(nc.vector.tensor_copy(lo[:, :], key_i[:, :]))
                link(nc.vector.memset(lo[HALF:HALF + 1, 0:OVERLAP], -1.0))
                link(nc.vector.tensor_scalar(key_i[:, :], nodes, HALF.bit_length() - 1, None,
                                             ALU.logical_shift_right))
                link(nc.vector.tensor_copy(hi[:, :], key_i[:, :]))

            def hot(base, trip, b, lo, hi):
                if not (base == 0 and isinstance(trip, int) and trip == 0):
                    v.wait_ge(s_cnt[b], base + trip)
                at = bass.ds(trip * (2 * C) + b * C, C)
                for t, ramp, part, w in ((hot_lo, ramp_lo, lo, HALF), (hot_hi, ramp_hi, hi, HC)):
                    nc.vector.tensor_tensor(t[b][:, :, :], ramp[:, :, :],
                                            part[:, at].unsqueeze(1).broadcast_to([P, w, C]),
                                            ALU.is_equal).then_inc(s_hot[b], 1)

            v.wait_ge(s_pool, 2)
            link(nc.vector.tensor_scalar(ident_b[:, :], ramp_f[:, :], part_f[:, 0:1], None, ALU.is_equal))
            link(nc.vector.tensor_copy(ident_h[:, :], ident_b[:, :]))
            nc.vector.tensor_scalar(ident[:, :], ramp_f[:, :], part_f[:, 0:1], None, ALU.is_equal).then_inc(s_const, 1)
            v.wait_ge(s_src, 32)
            split(src_i[:, 0:SLOTS], src_lo, src_hi)
            v.wait_ge(s_pool, 4)
            for b in range(2):
                hot(0, 0, b, src_lo, src_hi)
            with v.Fori(1, PAIRS) as trip:
                for b in range(2):
                    hot(0, trip, b, src_lo, src_hi)
            link(nc.vector.tensor_scalar(src_c[:, :], src_i[:, 0:SLOTS], -float(CENTER), None, ALU.add))
            v.wait_ge(s_cnt64, 1)
            nc.vector.tensor_copy(deg64[:, :], hist).then_inc(s_deg64, 1)
            v.wait_ge(s_deg, 1)
            nc.vector.tensor_scalar(deg_out[:, :], deg_ps, 1.0, None, ALU.max).then_inc(s_clip, 1)

            def stage(layer, b):
                nc.vector.tensor_copy(idx[b][:, :], LAYER_ROWS[layer][:, b * C:(b + 1) * C]).then_inc(s_idx[b], 1)

            stage(0, 0)
            stage(0, 1)
            v.wait_ge(s_sqrt, 1)
            link(nc.vector.reciprocal(out_scale[:, :], out_sqrt[:, :]))
            v.wait_ge(s_x, 32)
            for g in range(NG):
                cols = slice(g * G, (g + 1) * G)
                nc.vector.tensor_tensor(side[:, cols, :], feats[:, cols, :], over_cols(out_scale[:, cols], G),
                                        ALU.mult).then_inc(s_scaled, 1)


            def split_parts(h, m, low, value, rest):
                link(nc.vector.tensor_copy(h, value))
                link(nc.vector.tensor_tensor(rest, value, h, ALU.subtract))
                link(nc.vector.tensor_copy(m, rest))
                return nc.vector.tensor_tensor(low, rest, m, ALU.subtract)

            def split_table(table):
                h, m, low = (table_parts[:, :, k * D:(k + 1) * D] for k in range(3))
                split_parts(h, m, low, table[:, :, :], resid[:, :, :]).then_inc(s_tparts, 1)

            for g in range(NG):
                v.wait_ge(s_scaled, g + 1)
            split_table(side)
            v.wait_ge(s_relc, 1)
            nc.vector.memset(keep[:, :, 0], 0.0).then_inc(s_zero, 1)
            v.wait_ge(s_pool, 6)
            v.wait_ge(s_dst, 64)
            nc.vector.tensor_tensor(same[:, 1:SLOTS], dst_i[:, 1:SLOTS], dst_i[:, 0:SLOTS - 1],
                                    ALU.is_equal).then_inc(s_same, 1)
            nc.vector.memset(same[:, 0:1], 0.0).then_inc(s_same, 1)
            v.wait_ge(s_same, 2)
            nc.vector.memset(same[HALF:HALF + 1, OVERLAP:OVERLAP + 1], 0.0).then_inc(s_same, 1)
            link(nc.vector.tensor_copy(last_dst[:, :], dst_i[:, SLOTS - 1:SLOTS]))
            link(nc.vector.tensor_tensor(goes_on[:, :], next_i[:, :], last_dst[:, :], ALU.is_equal))
            link(nc.vector.tensor_scalar(carry_hot[:, :], carry_hot[:, :], last_dst[:, 0:1], goes_on[:, 0:1],
                                         ALU.is_equal, ALU.mult))
            link(nc.vector.tensor_scalar(upper[:, :], ramp_f[:, :], part_f[:, 0:1], None, ALU.is_ge))
            split(dst_i[:, :], dst_lo, dst_hi)
            v.wait_ge(s_typ, 64)
            for rows, rel in ((rows2, R2), (rows3, R3)):
                link(nc.vector.tensor_scalar(key_i[:, :], src_i[:, 0:SLOTS], rel.bit_length() - 1, None,
                                             ALU.logical_shift_left))
                link(nc.vector.tensor_tensor(rows[:, 0:SLOTS], rows[:, 0:SLOTS], key_i[:, :], ALU.add))
            v.wait_ge(s_par, PARAMS)
            link(nc.vector.tensor_scalar(eps1p[:, :], eps_sb[:, :], 1.0, None, ALU.add))
            v.wait_ge(s_same, 3)

            def place(layer, trip, b, j):
                n = pick_number(layer, trip, b)
                v.wait_ge(s_mul, PICKS * n + 2 * j + 2)
                at = (C - PICKS + 2 * j) * D
                nc.vector.tensor_reduce(got[b][:, at:at + 2 * D].rearrange("p (s f) -> p s f", f=D),
                                        picked(pair_number(b, j)).rearrange("p s k f -> p s f k"),
                                        AX.X, ALU.add).then_inc(s_filled, 1)

            def select(layer, trip, b, slots):
                n = pick_number(layer, trip, b)
                if slots[0] == 0:
                    v.wait_ge(s_rep, n + 1)
                for i in slots:
                    j, s = i // 2, i % 2
                    if i >= HOTS or not (isinstance(n, int) and n == 0):
                        v.wait_ge(s_mul, PICKS * n + i - HOTS + 1)
                    nc.vector.tensor_tensor(
                        hot_src[i % HOTS], node_rows[:, i, :].unsqueeze(1)
                        .broadcast_to([P, COLS, P]), ramp_src, ALU.is_equal).then_inc(s_sel, 1)
                    if s == 1 and j:
                        place(layer, trip, b, j - 1)

            def chunks(layer):
                def body(trip):
                    n = layer * PAIRS + trip
                    for b in range(2):
                        at = bass.ds(trip * (2 * C) + b * C, C)
                        if layer < 2 and isinstance(trip, int) and (trip, b) == (0, 0):
                            select(layer, *following(layer, trip, b), range(PICKS))
                        if not whole(layer, trip, b):
                            place(layer, trip, b, NPP - 1)
                            v.wait_ge(s_filled, NPP * (pick_number(layer, trip, b) + 1))
                        v.wait_ge(s_got[b], rows_in(layer, trip, b))
                        if not first(layer, trip):
                            v.wait_ge(s_run[b], n)
                        rows = got[b][:, :].rearrange("p (t f) -> p t f", f=D)
                        msg = msgT[b][:, :, :].rearrange("p f t -> p t f")
                        if layer in (0, 3):
                            nc.vector.tensor_tensor(msg, rows, weights[:, at].unsqueeze(2).broadcast_to([P, C, D]),
                                                    ALU.mult).then_inc(s_used[b], 1)
                        elif layer == 1:
                            v.wait_ge(s_aps, 2 * trip + b + 1)
                            nc.vector.tensor_tensor(msg, rows, attr_ps.rearrange("p (t f) -> p t f", f=D),
                                                    ALU.add).then_inc(s_used[b], 1)
                        nc.vector.tensor_copy(idx[b][:, :], LAYER_ROWS[layer][
                            :, bass.ds(trip * (2 * C) + (2 + b) * C, C)]).then_inc(s_idx[b], 1)
                        v.wait_ge(s_used[b], n + 1)
                        if following(layer, trip, b) and not whole(layer, trip, b):
                            select(layer, *following(layer, trip, b), range(1, PICKS))
                        if layer == 1:
                            v.wait_ge(s_moved[b], trip + 1)
                        if b or not first(layer, trip):
                            v.wait_ge(s_scan[1 - b], n + b)
                        nc.vector.scalar_tensor_tensor(
                            msgT[b][:, :, 0], msgT[1 - b][:, :, C - 1], same[:, bass.ds(trip * (2 * C) + b * C, 1)],
                            msgT[b][:, :, 0], ALU.mult, ALU.add).then_inc(s_mixed, 1)
                        v.wait_ge(s_mixed, 2 * n + b + 1)
                        v.wait_ge(s_keep, 2 * n + b + 1)
                        for f in range(0, D, KF):
                            some = msgT[b][:, f:min(f + KF, D), :].rearrange("p f t -> p (f t)")
                            last = nc.vector.tensor_tensor_scan(
                                some, keep[:, 0:min(KF, D - f), :].rearrange("p f t -> p (f t)"), some,
                                0.0, ALU.mult, ALU.add)
                        last.then_inc(s_scan[b], 1)
                        if layer == 0:
                            hot(PAIRS, trip, b, dst_lo, dst_hi)
                        if following(layer, trip, b) and following(layer, *following(layer, trip, b)):
                            select(layer, *following(layer, *following(layer, trip, b)), [0])

                if layer in (0, 3):
                    v.wait_ge(s_wps, 1 if layer == 0 else 2)
                v.wait_ge(s_pool, 7)
                trips(v, layer, body)
                v.wait_ge(s_scan[1], (layer + 1) * PAIRS)
                nc.vector.tensor_copy(tail_sum[:, :], msgT[1][:, :, C - 1]).then_inc(s_tail, 1)

            def degrees():
                v.wait_ge(s_cnt64, 2)
                nc.vector.tensor_copy(deg64[:, :], hist).then_inc(s_deg64, 1)
                v.wait_ge(s_deg, 2)
                link(nc.vector.tensor_copy(deg_in[:, :], deg_ps))
                nc.vector.tensor_scalar(in_clip[:, :], deg_in[:, :], 1.0, None, ALU.max).then_inc(s_clip, 1)
                link(nc.vector.tensor_scalar(has_in[:, :], deg_in[:, :], 1.0, None, ALU.min))
                v.wait_ge(s_clip, 2)
                link(nc.vector.reciprocal(in_inv[:, :], in_clip[:, :]))
                v.wait_ge(s_cum, 1)
                link(nc.vector.tensor_copy(col_tot[:, :], tot_ps))
                link(nc.vector.tensor_tensor_scan(col_cum[:, :], ones[:, 0:COLS], col_tot[:, :], -1.0,
                                                  ALU.mult, ALU.add))
                link(nc.vector.tensor_tensor(col_cum[:, :], col_cum[:, :], col_tot[:, :], ALU.subtract))
                link(nc.vector.tensor_tensor(end_f[:, :], cum_ps, col_cum[:, :], ALU.add))
                link(nc.vector.tensor_scalar(end_f[:, :], end_f[:, :], 0.0, None, ALU.max))
                link(nc.vector.tensor_scalar(end_up[:, :], end_f[:, :], float(E_HALF), float(OVERLAP),
                                             ALU.is_ge, ALU.mult))
                link(nc.vector.tensor_tensor(end_f[:, :], end_f[:, :], end_up[:, :], ALU.add))
                link(nc.vector.scalar_tensor_tensor(end_f[:, :], end_f[:, :], float(P * SLOTS), has_in[:, :],
                                                    ALU.subtract, ALU.mult))
                nc.vector.tensor_scalar(end_i[:, :], end_f[:, :], float(P * SLOTS), None, ALU.add)\
                    .then_inc(s_endi, 1)
                v.wait_ge(s_sqrt, 2)
                link(nc.vector.reciprocal(in_scale[:, :], in_sqrt[:, :]))

            def sum_ends(layer, g):
                q = layer * NG + g
                cols = slice(g * G, (g + 1) * G)
                a = agg[q % 2][:, :]
                v.wait_ge(s_end[g], 16 * G * (layer + 1))
                if q >= 2 and layer < 2:
                    v.wait_ge(s_turn, q - 1)
                if g == 0:
                    v.wait_ge(s_csum, layer + 1)
                ends = ends_sum[:, cols, :].rearrange("p c f -> p (c f)")
                add = nc.vector.tensor_tensor(a, ends, side[:, cols, :].rearrange("p c f -> p (c f)"), ALU.add)
                if layer in (0, 2):
                    link(add)
                    scale = in_scale if layer == 0 else in_inv
                    add = nc.vector.tensor_tensor(cube(a), cube(a), over_cols(scale[:, cols], G), ALU.mult)
                add.then_inc(s_agg, 1)

            def finish(layer, g):
                q = layer * NG + g
                cols = slice(g * G, (g + 1) * G)
                f = feats[:, cols, :]
                a = agg[q % 2][:, :]
                flat = f.rearrange("p c f -> p (c f)")
                if layer < 3:
                    v.wait_ge(s_lin, q + 1)
                if layer in (0, 2):
                    link(nc.vector.tensor_tensor(ta[:, :], lin_ps(q), resid[:, cols, :].rearrange("p c f -> p (c f)"),
                                                 ALU.add))
                if layer == 2:
                    link(nc.vector.tensor_tensor(ta[:, :], ta[:, :], a, ALU.add))
                if layer == 1:
                    link(nc.vector.tensor_tensor(cube(ta[:, :]), cube(lin_ps(q)),
                                                 bias[layer][:, :].unsqueeze(1).broadcast_to([P, G, D]), ALU.add))
                    link(nc.vector.scalar_tensor_tensor(ta[:, :], ta[:, :], 0.0, flat, ALU.max, ALU.add))
                if layer == 3:
                    v.wait_ge(s_agg, q + 1)
                    link(nc.vector.scalar_tensor_tensor(ta[:, :], a, 0.0, flat, ALU.max, ALU.add))
                link(nc.vector.tensor_reduce(row_sum[:, :], cube(ta[:, :]), AX.X, ALU.add))
                link(nc.vector.tensor_scalar(row_mean[:, :], row_sum[:, :], 1.0 / D, None, ALU.mult))
                link(nc.vector.tensor_tensor(cube(tb[:, :]), cube(ta[:, :]), over_cols(row_mean[:, :], G),
                                             ALU.subtract))
                link(nc.vector.tensor_tensor(ta[:, :], tb[:, :], tb[:, :], ALU.mult))
                link(nc.vector.tensor_reduce(row_sq[:, :], cube(ta[:, :]), AX.X, ALU.add))
                nc.vector.tensor_scalar(row_var[:, :], row_sq[:, :], 1.0 / D, LN_EPS, ALU.mult, ALU.add)\
                    .then_inc(s_var, 1)
                v.wait_ge(s_std, q + 1)
                link(nc.vector.reciprocal(row_inv[:, :], row_std[:, :]))
                nc.vector.tensor_tensor(f, cube(tb[:, :]), over_cols(row_inv[:, :], G), ALU.mult).then_inc(s_new, 1)
                v.wait_ge(s_new, q + 1)

            def feature_parts(layer, g):
                q = layer * NG + g
                if q > NG:
                    v.wait_ge(s_xt, q - NG)
                f = feats[:, g * G:(g + 1) * G, :]
                link(split_parts(part_hm[:, :, 0:D], part_hm[:, :, D:2 * D], part_hl[:, :, D:2 * D], f,
                                 cube(ta[:, :])))
                nc.vector.tensor_copy(part_hl[:, :, 0:D], part_hm[:, :, 0:D]).then_inc(s_parts, 1)

            for layer in range(4):
                if layer:
                    stage(layer, 0)
                    stage(layer, 1)
                if layer == 1:
                    split_table(feats)
                if layer:
                    if layer > 1:
                        v.wait_ge(s_yc, halves_before(layer, COLS))
                    nc.vector.memset(keep[:, :, 0], 0.0).then_inc(s_zero, 1)
                if layer in (0, 2):
                    nc.vector.tensor_tensor(resid[:, :, :], feats[:, :, :],
                                            bias[layer][:, :].unsqueeze(1).broadcast_to([P, COLS, D]),
                                            ALU.add).then_inc(s_resid, 1)
                chunks(layer)
                if layer in (0, 2):
                    v.wait_ge(s_resid, 1 + layer // 2)
                if layer == 0:
                    degrees()
                if layer == 1:
                    v.wait_ge(s_carry, 2)
                    nc.vector.scalar_tensor_tensor(
                        side[:, :, :].rearrange("p c f -> p (c f)"), feats[:, :, :].rearrange("p c f -> p (c f)"),
                        eps1p[:, 0:1], carry_ps, ALU.mult, ALU.add).then_inc(s_csum, 1)
                    v.wait_ge(s_csum, 2)
                sum_ends(layer, 0)
                for g in range(NG):
                    if g + 1 < NG:
                        sum_ends(layer, g + 1)
                    finish(layer, g)
                    if layer in (1, 2):
                        feature_parts(layer, g)


_INS = ['x', 'src', 'dst', 'edge_attr_64', 'edge_type_16', 'edge_type_32', 'edge_weight', 'edge_weight1',
        'L0_gnn_W', 'L0_gnn_b', 'L1_gnn_W', 'L1_gnn_b', 'L1_gnn_eps', 'L2_gnn_basis', 'L2_gnn_coeff',
        'L2_gnn_self_weight', 'L2_gnn_bias', 'L3_gnn_weight']
_OUTS = [((3125, 64), 'float32')]


def kernel(**inputs):
    import numpy as _np
    import concourse.bacc as _bacc
    from concourse import mybir as _mybir
    from concourse.bass_utils import run_bass_kernel_spmd as _run

    nc = _bacc.Bacc("TRN2", target_bir_lowering=False, num_devices=1)
    arrays, args = {}, []
    for name in _INS:
        a = _np.ascontiguousarray(inputs[name])
        if a.ndim == 0:
            a = a.reshape(1)
        arrays[f"in_{name}_dram"] = a
        args.append(nc.dram_tensor(f"in_{name}_dram", a.shape, _mybir.dt.from_np(a.dtype), kind="ExternalInput").ap())
    for i, (shape, dtype) in enumerate(_OUTS):
        dt = _mybir.dt.from_np(_np.dtype(dtype))
        args.append(nc.dram_tensor(f"out_{i}_dram", shape, dt, kind="ExternalOutput").ap())
    gnn_stack(nc, *args)
    r = _run(nc, [arrays], core_ids=[0])
    got = tuple(r.results[0][f"out_{i}_dram"] for i in range(len(_OUTS)))
    return got[0]
```

```python
import concourse.bass as bass
from concourse import mybir
from contextlib import ExitStack


def gnn_stack(nc, x, src, dst, edge_attr, etype16, etype32, weight0, weight3,
              W0, b0, W1, b1, eps1, basis, coeff, self_w, b2, W3, out):
    fp32, bf16, i32, fp16 = mybir.dt.float32, mybir.dt.bfloat16, mybir.dt.int32, mybir.dt.float16
    ALU, ACT, AX = mybir.AluOpType, mybir.ActivationFunctionType, mybir.AxisListType

    P = 128
    N, D = x.shape
    E = src.shape[0]
    R2, NB = coeff.shape
    R3 = W3.shape[0]
    HALF = P // 2
    SLOTS = -(-E // P)
    E_HALF = HALF * SLOTS
    HI0 = E - E_HALF
    OVERLAP = E_HALF - HI0
    C = 23
    PAIRS = SLOTS // (2 * C)
    assert PAIRS * 2 * C == SLOTS
    COLS = -(-N // P)
    NPAD = COLS * P
    LASTROWS = N - (COLS - 1) * P
    G = 5
    NG = COLS // G
    GW = G * D
    HC = 2 * COLS
    HCH = COLS
    LN_EPS = 1e-5
    BANK = 512
    KF = BANK // C
    PICKS = 6
    ALL_PICKS = [PICKS, PICKS, 2, 3]
    NPP = PICKS // 2
    CENTER = NPAD // 2
    HOTS = 3
    REL_HOTS = {2: 2, 3: 3}
    AHEAD = {2: 1, 3: 2}
    PICKED_CHUNKS = 2 * PAIRS - 1
    PARAMS = 16 * 10
    INITS = 8
    INEXACT = dict(allow_small_or_imprecise_dtypes=True)

    Y = 3

    def stored(n, y):
        return (n + Y - 1 - y) // Y

    def whole(trip, b):
        return isinstance(trip, int) and (trip, b) == (0, 0)

    def rows_in(layer, trip, b):
        before = sum((C - k) * PAIRS + (0 if b else k) for k in ALL_PICKS[:layer])
        some, extra = C - ALL_PICKS[layer], (0 if b else ALL_PICKS[layer])
        return 16 * (some * trip + (some + extra + before))

    assert NG * G == COLS and COLS == 25 and PICKS % 2 == 0 and PICKS % HOTS == 0 and PICKS > HOTS and CENTER <= 2048

    def dram(name, shape):
        return nc.dram_tensor(name, shape, fp32, kind="Internal").ap()

    table0 = dram("table0", [NPAD, D])
    table1 = dram("table1", [NPAD, D])
    table2 = dram("table2", [NPAD * R2, D])
    table3 = dram("table3", [NPAD * R3, D])
    sums = dram("running_sums", [P * SLOTS + 1, D])
    tables = [table0, table1, table2, table3]
    sums_pt = sums[0:P * SLOTS, :].rearrange("(p t) f -> p (t f)", t=SLOTS)

    def by_col(table):
        return table.rearrange("(c p) f -> p c f", p=P)

    def halves(vec):
        return (vec[0:E_HALF].rearrange("(p t) -> p t", t=SLOTS),
                vec[HI0:E].rearrange("(p t) -> p t", t=SLOTS))

    attr_lo = edge_attr[0:E_HALF, :].rearrange("(p t) f -> p (t f)", t=SLOTS)
    attr_hi = edge_attr[HI0:E, :].rearrange("(p t) f -> p (t f)", t=SLOTS)

    ctx = ExitStack()
    with ctx:
        def sb(name, shape, dt=fp32):
            return ctx.enter_context(nc.sbuf_tensor(name, shape, dt))

        def sem(name):
            return ctx.enter_context(nc.semaphore(name))

        src_i = sb("src_i", [P, SLOTS + 2 * C], i32)
        dst_i = sb("dst_i", [P, SLOTS], i32)
        rows2 = sb("rows2", [P, SLOTS + 2 * C], i32)
        rows3 = sb("rows3", [P, SLOTS + 2 * C], i32)
        key_i = sb("key_i", [P, SLOTS], i32)
        src_lo, src_hi, dst_lo, dst_hi = (sb(n, [P, SLOTS], bf16) for n in ("src_lo", "src_hi", "dst_lo", "dst_hi"))
        edge_w = sb("edge_w", [P, SLOTS])
        same = sb("same", [P, SLOTS])
        idx = [sb(f"idx{b}", [P, C], i32) for b in range(2)]
        got = [sb(f"got{b}", [P, C * D]) for b in range(2)]
        attr_mem = sb("attr_mem", [P, 2 * C * D])
        attr = [attr_mem[:, b * C * D:(b + 1) * C * D] for b in range(2)]
        masked = attr_mem[:, 0:R2 * D].rearrange("p (r f) -> p r f", f=D)
        msgT = [sb(f"msgT{b}", [P, D, C]) for b in range(2)]
        run = [sb(f"run{b}", [P, C * D]) for b in range(2)]
        HIST = (HALF + HC) * C
        hist_mem = sb("hist_mem", [P, 3 * HIST], bf16)

        def hist_low(n):
            return hist_mem[:, n * HIST:n * HIST + HALF * C].rearrange("p (w t) -> p w t", t=C)

        def hist_high(n):
            return hist_mem[:, n * HIST + HALF * C:(n + 1) * HIST].rearrange("p (w t) -> p w t", t=C)

        hot_lo, hot_hi = [hist_low(0), hist_low(1)], [hist_high(0), hist_high(1)]
        ramp_lo = hist_low(2)
        ramp_hi = hist_high(2)
        src_c = sb("src_c", [P, SLOTS], fp16)
        node_base = sb("node_base", [P, COLS], fp16)
        pick_type_i = sb("pick_type_i", [P, 3], i32)
        pick_type = sb("pick_type", [P, 3])
        pick_mask = sb("pick_mask", [P, 3, R2])
        picked_T = [sb(f"picked_T{b}", [P, 2, P], bf16) for b in range(2)]
        ident_h = sb("ident_h", [P, P], fp16)
        ramp_f = sb("ramp_f", [P, P])
        part_f = sb("part_f", [P, 1])
        ident = sb("ident", [P, P])
        ident_b = sb("ident_b", [P, P], bf16)
        upper = sb("upper", [P, P])
        ones = sb("ones", [P, P])
        zero_b = sb("zero_b", [P, HALF], bf16)
        feats = sb("feats", [P, COLS, D])
        side = sb("side", [P, COLS, D])
        aggT = sb("aggT", [D, G * P])
        part_hm = sb("part_hm", [P, G, 2 * D], bf16)
        part_hl = sb("part_hl", [P, G, 2 * D], bf16)
        parts = sb("parts", [P, 2 * NPAD], bf16)
        hmT, hlT = parts[:, 0:NPAD], parts[:, NPAD:2 * NPAD]
        table_parts = [m[:, 0:COLS * 3 * D].rearrange("p (c f) -> p c f", f=3 * D)
                       for m in (parts, hist_mem, hist_mem, hist_mem)]
        ends_sum = sb("ends_sum", [P, COLS, D])
        zero_row = sb("zero_row", [1, D])
        resid = sb("resid", [P, COLS, D])
        tail_sum = sb("tail_sum", [P, D])
        carry_hot = sb("carry_hot", [P, NPAD])
        next_i = sb("next_i", [P, 1], i32)
        last_dst, goes_on, eps_sb, eps1p = (sb(n, [P, 1]) for n in ("last_dst", "goes_on", "eps_sb", "eps1p"))
        (deg_out, out_sqrt, out_scale, deg_in, has_in, in_clip, in_sqrt, in_scale, in_inv, col_tot, col_cum,
         end_f, end_up) = (sb(n, [P, COLS]) for n in (
             "deg_out", "out_sqrt", "out_scale", "deg_in", "has_in", "in_clip", "in_sqrt", "in_scale",
             "in_inv", "col_tot", "col_cum", "end_f", "end_up"))
        deg64 = sb("deg64", [HALF, HC])
        end_i = sb("end_i", [P, COLS], i32)
        ta = sb("ta", [P, GW])
        tb = sb("tb", [P, GW])
        agg = [sb(f"agg{b}", [P, GW]) for b in range(2)]
        row_sum, row_mean, row_sq, row_var, row_std, row_inv = (
            sb(n, [P, G]) for n in ("row_sum", "row_mean", "row_sq", "row_var", "row_std", "row_inv"))
        w_raw = sb("w_raw", [D, 2, D])
        wT = sb("wT", [D, 2, D])
        sw_sb = sb("sw_sb", [P, D])
        rel3_sb = sb("rel3_sb", [P, R3 * D])
        bias = [sb(f"bias{l}", [P, D]) for l in range(3)]
        coeff_sb = sb("coeff_sb", [R2, NB])
        coeffT = sb("coeffT", [NB, R2])
        rel2, rel3, self3 = ([sb(f"{n}_{part}", [P, w], bf16) for part in ("h", "m", "x")]
                             for n, w in (("rel2", R2 * D), ("rel3", R3 * D), ("self", D)))
        ytiles = sb("ytiles", [P, Y, R2 * D])
        basis_sb = ytiles[0:NB, 0:2, :].rearrange("b a n -> b (a n)")
        rel2_sb = ytiles[:, 2, :]

        def in_ytile(y, dt):
            return ytiles[:, y, 0:COLS * P // 2].bitcast(dt).rearrange("p (c e) -> p c e", e=P)

        hot_src = [in_ytile(0, bf16), in_ytile(1, bf16),
                   ends_sum[:, :, :].rearrange("p c f -> p (c f)").bitcast(bf16).rearrange("p (c e) -> p c e", e=P)]
        ramp_src = in_ytile(2, fp16)

        psA = ctx.enter_context(nc.psum_tensor("psA", [P, 4 * BANK], fp32))
        psB = ctx.enter_context(nc.psum_tensor("psB", [P, 4 * BANK], fp32))
        keep = psB[:, 0:KF * C].rearrange("p (f t) -> p f t", t=C)
        weights = psA[:, 0:SLOTS]
        attr_ps = psA[:, 0:C * D]
        node_rows = psB[:, BANK:BANK + PICKS * P // 2].bitcast(fp16).rearrange("p (s e) -> p s e", e=P)

        def picked(at):
            return psB[:, (2 + at % 2) * BANK:(2 + at % 2) * BANK + 6 * D].rearrange("p (s k f) -> p s k f", s=2, k=3)

        def picked_ps(at):
            return psA[:, (2 + at % 2) * BANK:(2 + at % 2) * BANK + 2 * P].rearrange("p (k e) -> p k e", k=2)

        def rel_ps(h):
            return (psB[:, 2 * BANK:4 * BANK], psA[:, 0:2 * BANK])[h]

        hist = psA[0:HALF, 3 * BANK:3 * BANK + HC]
        deg_ps = psA[:, 2 * BANK + 2 * D:2 * BANK + 2 * D + HCH]
        cum_ps = psA[:, 2 * BANK:2 * BANK + COLS]
        tot_ps = psA[:, 2 * BANK + D:2 * BANK + D + COLS]
        carry_ps = psB[:, 0:COLS * D]
        turn_ps = psA[0:D, 2 * BANK:2 * BANK + G * P]
        turn_parts = psA[:, 2 * BANK:2 * BANK + G * P].bitcast(bf16).rearrange("p (k n) -> p k n", k=2)

        def lin_ps(q):
            return psA[:, (q % 2) * BANK:(q % 2) * BANK + GW]

        def y_ps(h):
            return psB[:, (h % 2) * 2 * BANK:(h % 2 + 1) * 2 * BANK]

        def over_cols(v, n):
            return v.unsqueeze(2).broadcast_to([P, n, D])

        def cube(t):
            return t.rearrange("p (c f) -> p c f", f=D)

        s_init = sem("buffers_cleared")
        s_src, s_dst, s_typ, s_w, s_x, s_par = (
            sem(n) for n in ("src_loaded", "dst_loaded", "types_loaded", "weights_loaded", "x_loaded",
                             "params_loaded"))
        s_basis = sem("basis_loaded")
        s_pool = sem("ramps_made")
        s_v = sem("vector_steps")
        s_const = sem("consts_ready")
        s_same = sem("segment_flags_ready")
        s_hot = [sem(f"hot_made{b}") for b in range(2)]
        s_cnt = [sem(f"hot_counted{b}") for b in range(2)]
        s_cnt64 = sem("degrees_counted")
        s_deg64 = sem("degrees_copied")
        s_deg = sem("degrees_spread")
        s_clip = sem("degrees_clipped")
        s_sqrt = sem("degree_sqrt_done")
        s_cum = sem("columns_summed")
        s_table = sem("table_stored")
        s_scaled = sem("scaled_ready")
        s_idx = [sem(f"idx_staged{b}") for b in range(2)]
        s_got = [sem(f"rows_gathered{b}") for b in range(2)]
        s_used = [sem(f"rows_used{b}") for b in range(2)]
        s_attr = [sem(f"attr_loaded{b}") for b in range(2)]
        s_mixed = sem("chunk_carried")
        s_keep = sem("keep_spread")
        s_resid = sem("residual_ready")
        s_zero = sem("keep_zeroed")
        s_wps = sem("weights_in_psum")
        s_aps = sem("attr_in_psum")
        s_relc = sem("relations_copied")
        s_ramp = sem("source_ramp_copied")
        s_rrep = sem("rel_nodes_replicated")
        s_type = sem("rel_types_ready")
        s_rsel = sem("rel_source_hots_made")
        s_rmul = sem("rel_features_picked")
        s_rcop = sem("rel_features_copied")
        s_prod = sem("rel_products_made")
        s_msk = sem("rel_products_masked")
        s_put = sem("rel_picks_placed")
        s_rel2 = sem("relations_doubled")
        s_pv = sem("pool_steps")
        s_tparts = sem("table_parts_ready")
        s_rep = sem("nodes_replicated")
        s_sel = sem("source_hots_made")
        s_mul = sem("slots_picked")
        s_filled = sem("picks_placed")
        s_relu = [sem(f"relu_done{b}") for b in range(2)]
        s_scan = [sem(f"chunk_scanned{b}") for b in range(2)]
        s_run = [sem(f"sums_copied{b}") for b in range(2)]
        s_wr = [sem(f"sums_stored{b}") for b in range(2)]
        s_zrow = sem("zero_row_stored")
        s_endi = sem("end_rows_ready")
        s_end = [sem(f"ends_gathered{g}") for g in range(NG)]
        s_tail = sem("tail_ready")
        s_carry = sem("carry_multiplied")
        s_agg = sem("agg_ready")
        s_turn = sem("agg_transposed")
        s_aggT = sem("aggT_copied")
        s_lin = sem("linear_done")
        s_new = sem("features_ready")
        s_var = sem("variance_ready")
        s_std = sem("std_ready")
        s_csum = sem("carry_copied")
        s_parts = sem("parts_ready")
        s_xt = sem("parts_transposed")
        s_xT = sem("parts_copied")
        s_wparts = sem("weight_parts_ready")
        s_wt = sem("weights_multiplied")
        s_wc = sem("weights_copied")
        s_y = sem("table_product")
        s_yc = sem("table_copied")
        s_yst = [sem(f"wide_table_stored{y}") for y in range(Y)]
        s_out = sem("output_stored")
        s_go = sem("chunk_started")

        LAYER_ROWS = [src_i, src_i, rows2, rows3]
        WIDE = {2: (R2, 0), 3: (R3, COLS)}

        def halves_before(layer, c):
            return 2 * c if layer == 2 else 2 * COLS + c

        def trips(eng, body):
            body(0)
            with eng.Fori(1, PAIRS - 1) as trip:
                body(trip)
            body(PAIRS - 1)

        def first(layer, trip):
            return layer == 0 and isinstance(trip, int) and trip == 0

        def following(trip, b):
            if isinstance(trip, int) and trip == PAIRS - 1 and b == 1:
                return None
            return (trip, 1) if b == 0 else (trip + 1, 0)

        def pick_number(layer, trip, b):
            return 2 * trip + (layer * PICKED_CHUNKS + b - 1)

        def rel_slots(layer, trip, b):
            k = ALL_PICKS[layer]
            return 2 * k * trip + (k * (b - 1) + (layer - 2) * ALL_PICKS[2] * PICKED_CHUNKS)

        def rel_halves(layer, trip, b):
            k = ALL_PICKS[layer] * HALVES[layer]
            return 2 * k * trip + (k * (b - 1) + (layer - 2) * ALL_PICKS[2] * HALVES[2] * PICKED_CHUNKS)

        def some(count):
            return not (isinstance(count, int) and count <= 0)

        HALVES = {2: R2 * D // (2 * BANK), 3: R3 * D // (2 * BANK)}

        def pair_number(layer, b, j):
            return NPP * (layer * PICKED_CHUNKS + b + 1) + j

        block = ctx.enter_context(nc.Block())

        @block.sync
        def _(sp):
            sp.wait_ge(s_init, INITS)
            for n, h in enumerate(halves(src)):
                sp.dma_start(src_i[n * HALF:(n + 1) * HALF, 0:SLOTS], h).then_inc(s_src, 16)
            sp.dma_start(feats[:, 0:COLS - 1, :], by_col(x[0:(COLS - 1) * P, :])).then_inc(s_x, 16)
            sp.dma_start(feats[0:LASTROWS, COLS - 1, :], x[(COLS - 1) * P:N, :]).then_inc(s_x, 16)
            for n, h in enumerate(halves(dst)):
                sp.dma_start(dst_i[n * HALF:(n + 1) * HALF, :], h).then_inc(s_dst, 16)
            after = dst[SLOTS:SLOTS + E_HALF].rearrange("(p t) -> p t", t=SLOTS)
            sp.dma_start(next_i[0:HALF, :], after[:, 0:1], allow_slow_non_contiguous=True).then_inc(s_dst, 16)
            after = dst[HI0 + SLOTS:E].rearrange("(p t) -> p t", t=SLOTS)
            sp.dma_start(next_i[HALF:P - 1, :], after[:, 0:1], allow_slow_non_contiguous=True).then_inc(s_dst, 16)

            def load_weights(v):
                for n, h in enumerate(halves(v)):
                    sp.dma_start(edge_w[n * HALF:(n + 1) * HALF, :], h).then_inc(s_w, 16)

            load_weights(weight0)
            for v, t in ((etype32, rows2), (etype16, rows3)):
                for n, h in enumerate(halves(v)):
                    sp.dma_start(t[n * HALF:(n + 1) * HALF, 0:SLOTS], h).then_inc(s_typ, 16)

            sp.dma_start(sums[P * SLOTS:P * SLOTS + 1, :], zero_row[:, :]).then_inc(s_zrow, 16)

            def store_sums(layer):
                def load_attr(b, at):
                    for n, half in enumerate((attr_lo, attr_hi)):
                        sp.dma_start(attr[b][n * HALF:(n + 1) * HALF, :],
                                     half[:, bass.ds(at, C * D)]).then_inc(s_attr[b], 16)

                def body(trip, last=False):
                    for b in range(2):
                        sp.wait_ge(s_run[b], layer * PAIRS + 1 + trip)
                        sp.dma_start(sums_pt[:, bass.ds(trip * (2 * C * D) + b * C * D, C * D)],
                                     run[b][:, :]).then_inc(s_wr[b], 16)
                        if layer == 1 and not last:
                            load_attr(b, trip * (2 * C * D) + (2 + b) * C * D)

                if layer == 1:
                    for b in range(2):
                        load_attr(b, b * C * D)
                with sp.Fori(0, PAIRS - 1) as trip:
                    body(trip)
                body(PAIRS - 1, last=True)

            def store_table(layer):
                if layer < 2:
                    for g in range(NG):
                        sp.wait_ge(*((s_scaled, g + 1) if layer == 0 else (s_new, g + 1)))
                        t = side if layer == 0 else feats
                        sp.dma_start(by_col(tables[layer])[:, g * G:(g + 1) * G, :],
                                     t[:, g * G:(g + 1) * G, :]).then_inc(s_table, 16)
                    return
                rel, before = WIDE[layer]
                wide = tables[layer].rearrange("(n r) f -> n (r f)", r=rel)
                for c in range(COLS):
                    sp.wait_ge(s_yc, halves_before(layer, c + 1))
                    y = (before + c) % Y
                    sp.dma_start(wide[c * P:(c + 1) * P, :], ytiles[:, y, 0:rel * D]).then_inc(s_yst[y], 16)

            for layer in range(4):
                store_table(layer)
                if layer == 0:
                    sp.wait_ge(s_wps, 1)
                    load_weights(weight3.rearrange("e o -> (e o)"))
                store_sums(layer)
            sp.wait_ge(s_new, 4 * NG)
            sp.dma_start(by_col(out[0:(COLS - 1) * P, :]), feats[:, 0:COLS - 1, :]).then_inc(s_out, 16)
            sp.dma_start(out[(COLS - 1) * P:N, :], feats[0:LASTROWS, COLS - 1, :]).then_inc(s_out, 16)
            sp.wait_ge(s_out, 32)

        @block.gpsimd
        def _(pool):
            made = [
                nc.gpsimd.iota(ramp_f[:, :], pattern=[[1, P]], base=0, channel_multiplier=0, **INEXACT),
                nc.gpsimd.iota(part_f[:, :], pattern=[[0, 1]], base=0, channel_multiplier=1, **INEXACT),
                nc.gpsimd.iota(ramp_lo, pattern=[[1, HALF], [0, C]], base=0, channel_multiplier=0, **INEXACT),
                nc.gpsimd.iota(ramp_hi, pattern=[[1, 2], [2, HCH], [0, C]], base=0, channel_multiplier=0,
                               **INEXACT),
                nc.gpsimd.iota(carry_hot[:, :], pattern=[[1, NPAD]], base=0, channel_multiplier=0, **INEXACT),
                nc.gpsimd.memset(ones[:, :], 1.0),
                nc.gpsimd.iota(node_base[:, :], pattern=[[P, COLS]], base=-CENTER, channel_multiplier=1, **INEXACT),
            ]
            for ins in made:
                ins.then_inc(s_pool, 1)

            steps = [0]

            def link(ins):
                steps[0] += 1
                ins.then_inc(s_pv, 1)
                pool.wait_ge(s_pv, steps[0])

            def weight_parts(w, value):
                cols = value.shape[1]
                low, high = slice(0, D), slice(D, P)
                rest = run[0]
                for at in range(0, cols, 2 * BANK):
                    n = min(2 * BANK, cols)
                    h, m, x = [t[:, at:at + n] for t in w]
                    link(nc.gpsimd.tensor_copy(h, value[:, at:at + n]))
                    link(nc.gpsimd.tensor_tensor(rest[:, 0:n], value[:, at:at + n], h, ALU.subtract))
                    link(nc.gpsimd.tensor_copy(m, rest[:, 0:n]))
                    link(nc.gpsimd.tensor_tensor(x[low], rest[low, 0:n], m[low], ALU.subtract))
                    link(nc.gpsimd.tensor_copy(x[high], h[high]))

            pool.wait_ge(s_par, PARAMS)
            weight_parts(self3, sw_sb[:, :])
            weight_parts(rel3, rel3_sb[:, :])
            pool.wait_ge(s_rel2, 16)
            weight_parts(rel2, rel2_sb)
            pool.sem_inc(s_wparts, 1)

            def gather_edges(layer):
                if layer < 2:
                    pool.wait_ge(s_table, 16 * NG * (layer + 1))
                else:
                    for y in range(Y):
                        pool.wait_ge(s_yst[y], 16 * stored(WIDE[layer][1] + COLS, y))

                def body(trip):
                    for b in range(2):
                        pool.wait_ge(s_idx[b], layer * (PAIRS + 1) + 1 + trip)
                        if not first(layer, trip):
                            pool.wait_ge(s_used[b], layer * PAIRS + trip)
                        pool.sem_inc(s_go, 1)
                        for s in range(C if whole(trip, b) else C - ALL_PICKS[layer]):
                            nc.gpsimd.indirect_dma_start(
                                out=got[b][:, s * D:(s + 1) * D], out_offset=None, in_=tables[layer],
                                in_offset=bass.IndirectOffsetOnAxis(ap=idx[b][:, s:s + 1], axis=0),
                            ).then_inc(s_got[b], 16)

                trips(pool, body)

            def gather_ends(layer):
                for b in range(2):
                    pool.wait_ge(s_wr[b], 16 * PAIRS * (layer + 1))
                pool.wait_ge(s_endi, 1)
                pool.wait_ge(s_zrow, 16)
                if layer:
                    pool.wait_ge(s_agg, NG * layer)
                for c in range(COLS):
                    nc.gpsimd.indirect_dma_start(
                        out=ends_sum[:, c, :], out_offset=None, in_=sums,
                        in_offset=bass.IndirectOffsetOnAxis(ap=end_i[:, c:c + 1], axis=0),
                    ).then_inc(s_end[c // G], 16)

            for layer in range(4):
                gather_edges(layer)
                gather_ends(layer)

        @block.scalar
        def _(act):
            act.wait_ge(s_init, INITS)
            act.dma_start(coeff_sb[:, :], coeff).then_inc(s_basis, 16)
            act.dma_start(basis_sb, basis.rearrange("b i o -> b (i o)")).then_inc(s_basis, 16)
            act.dma_start(w_raw[:, 0, :], W0).then_inc(s_par, 16)
            act.dma_start(w_raw[:, 1, :], W1).then_inc(s_par, 16)
            for t, v in zip(bias, (b0, b1, b2)):
                act.dma_start(t[:, :], v.unsqueeze(0).broadcast_to([P, D])).then_inc(s_par, 16)
            act.dma_start(eps_sb[:, :], eps1.unsqueeze(0).broadcast_to([P, 1])).then_inc(s_par, 16)
            for h in range(2):
                half = slice(h * D, (h + 1) * D)
                act.dma_start(sw_sb[half, :], self_w).then_inc(s_par, 16)
                act.dma_start(rel3_sb[half, :].rearrange("i (r o) -> i r o", r=R3),
                              W3.rearrange("r i o -> i r o")).then_inc(s_par, 16)
            act.wait_ge(s_wt, 2)
            nc.scalar.copy(wT[:, :, :], psA[0:D, 0:2 * D].rearrange("i (l o) -> i l o", l=2)).then_inc(s_wc, 1)
            act.wait_ge(s_wt, 3)
            nc.scalar.copy(rel2_sb[0:D, :].rearrange("i (r o) -> i o r", r=R2),
                           psB[0:D, :].rearrange("i (o r) -> i o r", r=R2)).then_inc(s_relc, 1)
            act.wait_ge(s_relc, 1)
            act.dma_start(rel2_sb[D:P, :], rel2_sb[0:D, :]).then_inc(s_rel2, 16)
            act.wait_ge(s_clip, 1)
            nc.scalar.activation(out_sqrt[:, :], deg_out[:, :], ACT.Sqrt).then_inc(s_sqrt, 1)
            act.wait_ge(s_same, 3)

            def spread(layer, trip, b):
                if b or not first(layer, trip):
                    act.wait_ge(s_scan[1 - b], layer * PAIRS + trip + b)
                nc.scalar.copy(keep[:, :, 1:C],
                               same[:, bass.ds(trip * (2 * C) + b * C + 1, C - 1)]
                               .unsqueeze(1).broadcast_to([P, KF, C - 1])).then_inc(s_keep, 1)

            def chunks(layer):
                act.wait_ge(s_zero, layer + 1)
                if layer in (0, 3):
                    act.wait_ge(s_w, 32 if layer == 0 else 64)
                    if layer == 0:
                        act.wait_ge(s_wc, 2)
                    nc.scalar.copy(weights, edge_w[:, :]).then_inc(s_wps, 1)

                if layer != 1:
                    act.wait_ge(s_wparts, 1)
                    act.wait_ge(s_pool, 7)
                    if layer:
                        for y in range(Y):
                            act.wait_ge(s_yst[y], 16 * stored(WIDE[layer][1] + COLS, y))
                    nc.scalar.copy(ramp_src, node_base[:, :].unsqueeze(2).broadcast_to([P, COLS, P]))\
                        .then_inc(s_ramp, 1)

                def copy_picked(trip, b):
                    slots = rel_slots(layer, trip, b)
                    halves = rel_halves(layer, trip, b)
                    for i in range(ALL_PICKS[layer]):
                        at = (ALL_PICKS[layer] * (b + 1) + i) % 2
                        act.wait_ge(s_rmul, slots + i + 1)
                        if some(halves + HALVES[layer] * (i - 1)):
                            act.wait_ge(s_prod, halves + HALVES[layer] * (i - 1))
                        nc.scalar.copy(picked_T[at][:, :, :], picked_ps(at)).then_inc(s_rcop, 1)

                def stage_attr(trip, b):
                    act.wait_ge(s_attr[b], 32 * (trip + 1))
                    act.wait_ge(s_used[1 - b], layer * PAIRS + trip + b)
                    nc.scalar.copy(attr_ps, attr[b]).then_inc(s_aps, 1)

                def body(trip):
                    n = layer * PAIRS + trip
                    for b in range(2):
                        next_chunk = (trip, 1) if b == 0 else (trip + 1, 0)
                        if b and isinstance(trip, int) and trip == PAIRS - 1:
                            next_chunk = None
                        if layer == 1:
                            if isinstance(trip, int) and trip == 0 and b == 0:
                                stage_attr(trip, b)
                                spread(layer, trip, b)
                            act.wait_ge(s_used[b], n + 1)
                            nc.scalar.activation(msgT[b][:, :, :], msgT[b][:, :, :], ACT.Relu)\
                                .then_inc(s_relu[b], 1)
                            if next_chunk:
                                stage_attr(*next_chunk)
                        elif layer == 2:
                            spread(layer, trip, b)
                            act.wait_ge(s_got[b], rows_in(layer, trip, b))
                            if not whole(trip, b):
                                act.wait_ge(s_put, rel_slots(layer, trip, b) + ALL_PICKS[layer])
                            nc.scalar.copy(msgT[b][:, :, :].rearrange("p f t -> p t f"),
                                           got[b][:, :].rearrange("p (t f) -> p t f", f=D)).then_inc(s_used[b], 1)
                        else:
                            spread(layer, trip, b)
                        if layer > 1 and following(trip, b):
                            copy_picked(*following(trip, b))
                        act.wait_ge(s_scan[b], n + 1)
                        if not first(layer, trip):
                            act.wait_ge(s_wr[b], n * 16)
                        nc.scalar.copy(run[b][:, :].rearrange("p (t f) -> p f t", f=D),
                                       msgT[b][:, :, :]).then_inc(s_run[b], 1)
                        if layer == 1 and next_chunk:
                            spread(layer, *next_chunk)

                trips(act, body)

            def nodes(layer):
                if layer == 0:
                    act.wait_ge(s_clip, 2)
                    nc.scalar.activation(in_sqrt[:, :], in_clip[:, :], ACT.Sqrt).then_inc(s_sqrt, 1)
                act.wait_ge(s_carry, layer + 1)
                if layer:
                    act.wait_ge(s_agg, NG * layer)
                else:
                    act.wait_ge(s_table, 16 * NG)
                if layer != 1:
                    nc.scalar.copy(side[:, :, :].rearrange("p c f -> p (c f)"), carry_ps).then_inc(s_csum, 1)

                def turned(g):
                    q = layer * NG + g
                    act.wait_ge(s_xt, q - NG + 1)
                    for k, t in enumerate((hmT, hlT)):
                        nc.scalar.copy(t[:, g * G * P:(g + 1) * G * P], turn_parts[:, k, :]).then_inc(s_xT, 1)

                def table(c):
                    rel, before = WIDE[layer + 1]
                    n = before + c
                    if n >= Y:
                        act.wait_ge(s_yst[n % Y], 16 * stored(n, n % Y))
                    for h in range(rel * D // (2 * BANK)):
                        y = halves_before(layer + 1, c) + h
                        act.wait_ge(s_y, y + 1)
                        nc.scalar.copy(ytiles[:, n % Y, h * 2 * BANK:(h + 1) * 2 * BANK], y_ps(y))\
                            .then_inc(s_yc, 1)

                def copy_aggT(g):
                    if layer < 2 and g < NG:
                        q = layer * NG + g
                        act.wait_ge(s_turn, q + 1)
                        if q:
                            act.wait_ge(s_lin, q)
                        nc.scalar.copy(aggT[:, :], turn_ps).then_inc(s_aggT, 1)

                def root(g):
                    if g < NG:
                        act.wait_ge(s_var, layer * NG + g + 1)
                        nc.scalar.activation(row_std[:, :], row_var[:, :], ACT.Sqrt).then_inc(s_std, 1)

                if layer in (0, 3):
                    for g in range(NG):
                        copy_aggT(g)
                        root(g)
                else:
                    copy_aggT(0)
                    copy_aggT(1)
                    root(0)
                    turned(0)
                    for g in range(NG):
                        c = g * G
                        table(c)
                        root(g + 1)
                        copy_aggT(g + 2)
                        table(c + 1)
                        table(c + 2)
                        if g + 1 < NG:
                            turned(g + 1)
                        table(c + 3)
                        table(c + 4)

            for layer in range(4):
                chunks(layer)
                nodes(layer)

        @block.tensor
        def _(pe):
            def count(base, trip, b):
                pe.wait_ge(s_hot[b], 2 * (base + trip) + 2)
                for s in range(C):
                    last = nc.tensor.matmul(hist, hot_lo[b][:, :, s], hot_hi[b][:, :, s],
                                            start=False, stop=False, skip_group_check=True)
                last.then_inc(s_cnt[b], 1)

            def count_sources(lo, hi):
                with pe.Fori(lo, hi) as trip:
                    for b in range(2):
                        count(0, trip, b)

            def pick(layer, trip, b):
                n = pick_number(layer, trip, b)
                start = isinstance(n, int) and n == 0

                def replicate(trip, b):
                    for i in range(PICKS):
                        slot = bass.ds(trip * (2 * C) + (b + 1) * C - PICKS + i, 1)
                        last = nc.tensor.transpose(node_rows[:, i, :], src_c[:, slot].broadcast_to([P, P]),
                                                   ident_h[:, :])
                    last.then_inc(s_rep, 1)

                if isinstance(trip, int) and trip == 0:
                    if not start:
                        pe.wait_ge(s_sel, PICKS * n)
                    replicate(trip, b)
                for j in range(NPP):
                    if j >= 2 or not start:
                        pe.wait_ge(s_filled, NPP * n + j - 1)
                    for s in range(2):
                        i = 2 * j + s
                        if i == PICKS - 2 and following(trip, b):
                            pe.wait_ge(s_sel, PICKS * (n + 1))
                            replicate(*following(trip, b))
                        pe.wait_ge(s_sel, PICKS * n + i + 1)
                        for c in range(COLS):
                            last = nc.tensor.matmul(
                                picked(pair_number(layer, b, j))[:, s, :, :].rearrange("p k f -> p (k f)"),
                                hot_src[i % HOTS][:, c, :], table_parts[layer][:, c, :], start=(c == 0), stop=(c == COLS - 1))
                        last.then_inc(s_mul, 1)

            def bound(start):
                last = nc.tensor.matmul(hist, zero_b[:, :], zero_b[:, 0:HC], start=start, stop=not start,
                                        skip_group_check=True)
                if not start:
                    last.then_inc(s_cnt64, 1)

            def spread_degrees(n):
                pe.wait_ge(s_deg64, n)
                for h in range(2):
                    last = nc.tensor.matmul(deg_ps[h * HALF:(h + 1) * HALF, :], ident[0:HALF, 0:HALF],
                                            deg64[:, h * HCH:(h + 1) * HCH], start=True, stop=True)
                last.then_inc(s_deg, 1)

            PARTS = 4

            def relations(part):
                for o in range(part * D // PARTS, (part + 1) * D // PARTS):
                    last = nc.tensor.matmul(psB[0:D, o * R2:(o + 1) * R2], basis_sb[:, o:D * D:D], coeffT[:, :],
                                            start=True, stop=True)
                return last

            pe.wait_ge(s_init, INITS)
            bound(True)
            pe.wait_ge(s_const, 1)
            pe.wait_ge(s_basis, 32)
            nc.tensor.transpose(psA[0:NB, BANK:BANK + R2], coeff_sb[:, :], ident[0:R2, 0:R2]).then_inc(s_wt, 1)
            pe.wait_ge(s_wc, 1)
            relations(0)
            count_sources(0, 3)
            pe.wait_ge(s_par, PARAMS)
            for l in range(2):
                last = nc.tensor.transpose(psA[0:D, l * D:(l + 1) * D], w_raw[:, l, :], ident[0:D, 0:D])
            last.then_inc(s_wt, 1)
            relations(1)
            count_sources(3, 6)
            relations(2)
            count_sources(6, 9)
            relations(3).then_inc(s_wt, 1)
            count_sources(9, PAIRS)
            bound(False)
            spread_degrees(1)
            bound(True)
            pe.wait_ge(s_tparts, 1)
            pe.wait_ge(s_relc, 1)

            def beside_chunks(trip):
                for b in range(2):
                    if following(trip, b):
                        pick(0, *following(trip, b))
                    count(PAIRS, trip, b)

            trips(pe, beside_chunks)
            bound(False)
            spread_degrees(2)
            pe.wait_ge(s_clip, 2)
            nc.tensor.matmul(cum_ps, upper[:, :], deg_in[:, :], start=True, stop=True)
            nc.tensor.matmul(tot_ps, ones[:, :], deg_in[:, :], start=True, stop=True).then_inc(s_cum, 1)

            def by_parts(out_ps, hm, hl, w, cols):
                for n, (x_part, w_part) in enumerate(((hm, w[0]), (hm, w[1]), (hl, w[2]))):
                    last = nc.tensor.matmul(out_ps, x_part, w_part[:, cols], start=(n == 0), stop=(n == 2))
                return last

            def pick_rel(layer, trip, b):
                K, H = ALL_PICKS[layer], HALVES[layer]
                slots, halves = rel_slots(layer, trip, b), rel_halves(layer, trip, b)
                w = rel2 if layer == 2 else rel3

                def replicate(trip, b):
                    for i in range(K):
                        slot = bass.ds(trip * (2 * C) + (b + 1) * C - K + i, 1)
                        last = nc.tensor.transpose(node_rows[:, i, :], src_c[:, slot].broadcast_to([P, P]),
                                                   ident_h[:, :])
                    last.then_inc(s_rrep, 1)

                if isinstance(trip, int) and trip == 0:
                    if some(slots):
                        pe.wait_ge(s_rsel, slots)
                    replicate(trip, b)

                def products(i):
                    at = (K * (b + 1) + i) % 2
                    pe.wait_ge(s_rcop, slots + i + 1)
                    for h in range(H):
                        if some(halves + H * (i - 1) + h + 1):
                            pe.wait_ge(s_msk, halves + H * (i - 1) + h + 1)
                        for k in range(2):
                            col = (2 * h + k) * BANK
                            last = by_parts(rel_ps(h)[:, k * BANK:(k + 1) * BANK], picked_T[at][:, 0, :],
                                            picked_T[at][:, 1, :], w, slice(col, col + BANK))
                        last.then_inc(s_prod, 1)

                for i in range(K):
                    at = (K * (b + 1) + i) % 2
                    pe.wait_ge(s_rsel, slots + i + 1)
                    if some(slots + i - 1):
                        pe.wait_ge(s_rcop, slots + i - 1)
                    for k in range(2):
                        for c in range(COLS):
                            last = nc.tensor.matmul(picked_ps(at)[:, k, :],
                                                    table_parts[layer][:, c, k * D:(k + 2) * D],
                                                    hot_src[i % REL_HOTS[layer]][:, c, :],
                                                    start=(c == 0), stop=(c == COLS - 1))
                    last.then_inc(s_rmul, 1)
                    if i == AHEAD[layer] - 1 and following(trip, b):
                        pe.wait_ge(s_rsel, slots + K)
                        replicate(*following(trip, b))
                    if i:
                        products(i - 1)
                products(K - 1)

            def nodes(layer):
                pe.wait_ge(s_tail, layer + 1)
                for c in range(COLS):
                    last = nc.tensor.matmul(carry_ps[:, c * D:(c + 1) * D], carry_hot[:, c * P:(c + 1) * P],
                                            tail_sum[:, :], start=True, stop=True)
                last.then_inc(s_carry, 1)

                def turn_sums(g):
                    if layer > 1 or g >= NG:
                        return
                    q = layer * NG + g
                    pe.wait_ge(s_agg, q + 1)
                    if q:
                        pe.wait_ge(s_aggT, q)
                    if layer == 1 and g >= 2:
                        pe.wait_ge(s_xT, 2 * (q - NG - 1))
                    for j in range(G):
                        last = nc.tensor.transpose(turn_ps[:, j * P:(j + 1) * P],
                                                   cube(agg[q % 2][:, :])[:, j, :], ident[:, :])
                    last.then_inc(s_turn, 1)

                def linear(g):
                    if layer > 2 or g >= NG:
                        return
                    q = layer * NG + g
                    if layer < 2:
                        pe.wait_ge(s_aggT, q + 1)
                    if q >= 2:
                        pe.wait_ge(s_new, q - 1)
                    for j in range(G):
                        out_ps = lin_ps(q)[:, j * D:(j + 1) * D]
                        if layer < 2:
                            last = nc.tensor.matmul(out_ps, aggT[:, j * P:(j + 1) * P], wT[:, layer, :],
                                                    start=True, stop=True)
                        else:
                            at = slice((g * G + j) * P, (g * G + j + 1) * P)
                            last = by_parts(out_ps, hmT[:, at], hlT[:, at], self3, slice(0, D))
                    last.then_inc(s_lin, 1)

                def turn_parts_of(g):
                    q = layer * NG + g
                    pe.wait_ge(s_parts, q - NG + 1)
                    if q > NG:
                        pe.wait_ge(s_xT, 2 * (q - NG))
                    if layer < 2:
                        pe.wait_ge(s_aggT, min(q + 2, NG * (layer + 1)))
                    for k, t in enumerate((part_hm, part_hl)):
                        for j in range(G):
                            last = nc.tensor.transpose(turn_parts[:, k, j * P:(j + 1) * P], t[:, j, :],
                                                       ident_b[:, :])
                    last.then_inc(s_xt, 1)

                def table(c):
                    pe.wait_ge(s_xT, 2 * (layer * NG + c // G - NG + 1))
                    rel, _ = WIDE[layer + 1]
                    w = rel2 if layer == 1 else rel3
                    for h in range(rel * D // (2 * BANK)):
                        y = halves_before(layer + 1, c) + h
                        if y >= 2:
                            pe.wait_ge(s_yc, y - 1)
                        for k in range(2):
                            col = (2 * h + k) * BANK
                            last = by_parts(y_ps(y)[:, k * BANK:(k + 1) * BANK], hmT[:, c * P:(c + 1) * P],
                                            hlT[:, c * P:(c + 1) * P], w, slice(col, col + BANK))
                        last.then_inc(s_y, 1)

                if layer in (0, 3):
                    for g in range(NG):
                        turn_sums(g)
                        linear(g)
                    return
                turn_sums(0)
                linear(0)
                turn_sums(1)
                linear(1)
                turn_parts_of(0)
                pe.wait_ge(s_csum, layer + 1)
                pe.wait_ge(s_wparts, 1)
                for g in range(NG):
                    c = g * G
                    table(c)
                    turn_sums(g + 2)
                    table(c + 1)
                    linear(g + 2)
                    table(c + 2)
                    if g + 1 < NG:
                        turn_parts_of(g + 1)
                    table(c + 3)
                    table(c + 4)

            for layer in range(4):
                if layer:
                    pe.wait_ge(s_tparts, layer + 1)
                    if layer > 1:
                        pe.wait_ge(s_yc, halves_before(layer, COLS))

                    def picks(trip):
                        for b in range(2):
                            if following(trip, b):
                                (pick if layer == 1 else pick_rel)(layer, *following(trip, b))

                    trips(pe, picks)
                nodes(layer)

        @block.vector
        def _(v):
            steps = [0]

            def link(ins):
                steps[0] += 1
                ins.then_inc(s_v, 1)
                v.wait_ge(s_v, steps[0])

            for t, value in ((src_i[:, SLOTS:], 0), (rows2[:, SLOTS:], 0), (rows3[:, SLOTS:], 0),
                             (feats[:, COLS - 1, :], 0.0), (next_i[:, :], -1), (zero_b[:, :], 0.0),
                             (msgT[1][:, :, C - 1], 0.0), (zero_row[:, :], 0.0)):
                nc.vector.memset(t, value).then_inc(s_init, 1)

            def split(nodes, lo, hi):
                link(nc.vector.tensor_scalar(key_i[:, :], nodes, HALF - 1, None, ALU.bitwise_and))
                link(nc.vector.tensor_copy(lo[:, :], key_i[:, :]))
                link(nc.vector.memset(lo[HALF:HALF + 1, 0:OVERLAP], -1.0))
                link(nc.vector.tensor_scalar(key_i[:, :], nodes, HALF.bit_length() - 1, None,
                                             ALU.logical_shift_right))
                link(nc.vector.tensor_copy(hi[:, :], key_i[:, :]))

            def hot(base, trip, b, lo, hi):
                if not (base == 0 and isinstance(trip, int) and trip == 0):
                    v.wait_ge(s_cnt[b], base + trip)
                at = bass.ds(trip * (2 * C) + b * C, C)
                for t, ramp, part, w in ((hot_lo, ramp_lo, lo, HALF), (hot_hi, ramp_hi, hi, HC)):
                    nc.vector.tensor_tensor(t[b], ramp,
                                            part[:, at].unsqueeze(1).broadcast_to([P, w, C]),
                                            ALU.is_equal).then_inc(s_hot[b], 1)

            v.wait_ge(s_pool, 2)
            link(nc.vector.tensor_scalar(ident_b[:, :], ramp_f[:, :], part_f[:, 0:1], None, ALU.is_equal))
            link(nc.vector.tensor_copy(ident_h[:, :], ident_b[:, :]))
            nc.vector.tensor_scalar(ident[:, :], ramp_f[:, :], part_f[:, 0:1], None, ALU.is_equal).then_inc(s_const, 1)
            v.wait_ge(s_src, 32)
            split(src_i[:, 0:SLOTS], src_lo, src_hi)
            v.wait_ge(s_wt, 1)
            nc.vector.tensor_copy(coeffT[:, :], psA[0:NB, BANK:BANK + R2]).then_inc(s_wc, 1)
            v.wait_ge(s_pool, 4)
            for b in range(2):
                hot(0, 0, b, src_lo, src_hi)
            with v.Fori(1, PAIRS) as trip:
                for b in range(2):
                    hot(0, trip, b, src_lo, src_hi)
            link(nc.vector.tensor_scalar(src_c[:, :], src_i[:, 0:SLOTS], -float(CENTER), None, ALU.add))
            v.wait_ge(s_cnt64, 1)
            nc.vector.tensor_copy(deg64[:, :], hist).then_inc(s_deg64, 1)
            v.wait_ge(s_deg, 1)
            nc.vector.tensor_scalar(deg_out[:, :], deg_ps, 1.0, None, ALU.max).then_inc(s_clip, 1)

            def stage(layer, b):
                nc.vector.tensor_copy(idx[b][:, :], LAYER_ROWS[layer][:, b * C:(b + 1) * C]).then_inc(s_idx[b], 1)

            stage(0, 0)
            stage(0, 1)
            v.wait_ge(s_sqrt, 1)
            link(nc.vector.reciprocal(out_scale[:, :], out_sqrt[:, :]))
            v.wait_ge(s_x, 32)
            for g in range(NG):
                cols = slice(g * G, (g + 1) * G)
                nc.vector.tensor_tensor(side[:, cols, :], feats[:, cols, :], over_cols(out_scale[:, cols], G),
                                        ALU.mult).then_inc(s_scaled, 1)


            def split_parts(h, m, low, value, rest):
                link(nc.vector.tensor_copy(h, value))
                link(nc.vector.tensor_tensor(rest, value, h, ALU.subtract))
                link(nc.vector.tensor_copy(m, rest))
                return nc.vector.tensor_tensor(low, rest, m, ALU.subtract)

            def split_table(layer, table):
                m, h, low = (table_parts[layer][:, :, k * D:(k + 1) * D] for k in range(3))
                split_parts(h, m, low, table[:, :, :], resid[:, :, :]).then_inc(s_tparts, 1)

            for g in range(NG):
                v.wait_ge(s_scaled, g + 1)
            split_table(0, side)
            v.wait_ge(s_relc, 1)
            nc.vector.memset(keep[:, :, 0], 0.0).then_inc(s_zero, 1)
            v.wait_ge(s_pool, 6)
            v.wait_ge(s_dst, 64)
            nc.vector.tensor_tensor(same[:, 1:SLOTS], dst_i[:, 1:SLOTS], dst_i[:, 0:SLOTS - 1],
                                    ALU.is_equal).then_inc(s_same, 1)
            nc.vector.memset(same[:, 0:1], 0.0).then_inc(s_same, 1)
            v.wait_ge(s_same, 2)
            nc.vector.memset(same[HALF:HALF + 1, OVERLAP:OVERLAP + 1], 0.0).then_inc(s_same, 1)
            link(nc.vector.tensor_copy(last_dst[:, :], dst_i[:, SLOTS - 1:SLOTS]))
            link(nc.vector.tensor_tensor(goes_on[:, :], next_i[:, :], last_dst[:, :], ALU.is_equal))
            link(nc.vector.tensor_scalar(carry_hot[:, :], carry_hot[:, :], last_dst[:, 0:1], goes_on[:, 0:1],
                                         ALU.is_equal, ALU.mult))
            link(nc.vector.tensor_scalar(upper[:, :], ramp_f[:, :], part_f[:, 0:1], None, ALU.is_ge))
            split(dst_i[:, :], dst_lo, dst_hi)
            v.wait_ge(s_typ, 64)
            for rows, rel in ((rows2, R2), (rows3, R3)):
                link(nc.vector.tensor_scalar(key_i[:, :], src_i[:, 0:SLOTS], rel.bit_length() - 1, None,
                                             ALU.logical_shift_left))
                link(nc.vector.tensor_tensor(rows[:, 0:SLOTS], rows[:, 0:SLOTS], key_i[:, :], ALU.add))
            v.wait_ge(s_par, PARAMS)
            link(nc.vector.tensor_scalar(eps1p[:, :], eps_sb[:, :], 1.0, None, ALU.add))
            v.wait_ge(s_same, 3)

            def place(layer, trip, b, j):
                n = pick_number(layer, trip, b)
                v.wait_ge(s_mul, PICKS * n + 2 * j + 2)
                at = (C - PICKS + 2 * j) * D
                nc.vector.tensor_reduce(got[b][:, at:at + 2 * D].rearrange("p (s f) -> p s f", f=D),
                                        picked(pair_number(layer, b, j)).rearrange("p s k f -> p s f k"),
                                        AX.X, ALU.add).then_inc(s_filled, 1)

            def select(layer, trip, b, slots):
                n = pick_number(layer, trip, b)
                if slots[0] == 0:
                    v.wait_ge(s_rep, n + 1)
                for i in slots:
                    j, s = i // 2, i % 2
                    if i >= HOTS or not (isinstance(n, int) and n == 0):
                        v.wait_ge(s_mul, PICKS * n + i - HOTS + 1)
                    nc.vector.tensor_tensor(
                        hot_src[i % HOTS], node_rows[:, i, :].unsqueeze(1)
                        .broadcast_to([P, COLS, P]), ramp_src, ALU.is_equal).then_inc(s_sel, 1)
                    if s == 1 and j:
                        place(layer, trip, b, j - 1)

            def select_rel(layer, trip, b, of):
                n = pick_number(layer - 2, trip, b)
                slots = rel_slots(layer, trip, b)
                if of[0] == 0:
                    v.wait_ge(s_rrep, n + 1)
                else:
                    relation_masks(layer, trip, b)
                for i in of:
                    if some(slots + i - REL_HOTS[layer] + 1):
                        v.wait_ge(s_rmul, slots + i - REL_HOTS[layer] + 1)
                    nc.vector.tensor_tensor(
                        hot_src[i % REL_HOTS[layer]], node_rows[:, i, :].unsqueeze(1)
                        .broadcast_to([P, COLS, P]), ramp_src, ALU.is_equal).then_inc(s_rsel, 1)

            def relation_masks(layer, trip, b):
                K, R = ALL_PICKS[layer], WIDE[layer][0]
                n = pick_number(layer - 2, trip, b)
                at = bass.ds(trip * (2 * C) + (b + 1) * C - K, K)
                nc.vector.tensor_scalar(pick_type_i[:, 0:K], LAYER_ROWS[layer][:, at], R - 1, None,
                                        ALU.bitwise_and).then_inc(s_type, 1)
                v.wait_ge(s_type, 3 * n + 1)
                nc.vector.tensor_copy(pick_type[:, 0:K], pick_type_i[:, 0:K]).then_inc(s_type, 1)
                v.wait_ge(s_type, 3 * n + 2)
                nc.vector.tensor_tensor(pick_mask[:, 0:K, 0:R], ramp_f[:, 0:R].unsqueeze(1).broadcast_to([P, K, R]),
                                        pick_type[:, 0:K].unsqueeze(2).broadcast_to([P, K, R]),
                                        ALU.is_equal).then_inc(s_type, 1)

            def place_rel(layer, trip, b):
                K, H, R = ALL_PICKS[layer], HALVES[layer], WIDE[layer][0]
                slots, halves = rel_slots(layer, trip, b), rel_halves(layer, trip, b)
                v.wait_ge(s_type, 3 * pick_number(layer - 2, trip, b) + 3)
                for i in range(K):
                    if some(slots + i):
                        v.wait_ge(s_put, slots + i)
                    for h in range(H):
                        v.wait_ge(s_prod, halves + H * i + h + 1)
                        half = slice(h * R // H, (h + 1) * R // H)
                        nc.vector.tensor_tensor(masked[:, half, :], cube(rel_ps(h)),
                                                over_cols(pick_mask[:, i, half], R // H), ALU.mult)\
                            .then_inc(s_msk, 1)
                    v.wait_ge(s_msk, halves + H * (i + 1))
                    to = (C - K + i) * D
                    nc.vector.tensor_reduce(got[b][:, to:to + D], masked[:, 0:R, :].rearrange("p r f -> p f r"),
                                            AX.X, ALU.add).then_inc(s_put, 1)

            def chunks(layer):
                def body(trip):
                    n = layer * PAIRS + trip
                    for b in range(2):
                        nxt = following(trip, b)
                        at = bass.ds(trip * (2 * C) + b * C, C)
                        if layer < 2 and nxt and whole(trip, b):
                            select(layer, *nxt, range(PICKS))
                        if layer > 1 and nxt and whole(trip, b):
                            select_rel(layer, *nxt, range(AHEAD[layer]))
                            select_rel(layer, *nxt, range(AHEAD[layer], ALL_PICKS[layer]))
                        if layer > 1 and not whole(trip, b):
                            v.wait_ge(s_put, rel_slots(layer, trip, b) + ALL_PICKS[layer])
                        if layer < 2 and not whole(trip, b):
                            place(layer, trip, b, NPP - 1)
                            v.wait_ge(s_filled, NPP * (pick_number(layer, trip, b) + 1))
                        v.wait_ge(s_got[b], rows_in(layer, trip, b))
                        if not first(layer, trip):
                            v.wait_ge(s_run[b], n)
                        rows = got[b][:, :].rearrange("p (t f) -> p t f", f=D)
                        msg = msgT[b][:, :, :].rearrange("p f t -> p t f")
                        if layer in (0, 3):
                            nc.vector.tensor_tensor(msg, rows, weights[:, at].unsqueeze(2).broadcast_to([P, C, D]),
                                                    ALU.mult).then_inc(s_used[b], 1)
                        elif layer == 1:
                            v.wait_ge(s_aps, 2 * trip + b + 1)
                            nc.vector.tensor_tensor(msg, rows, attr_ps.rearrange("p (t f) -> p t f", f=D),
                                                    ALU.add).then_inc(s_used[b], 1)
                        nc.vector.tensor_copy(idx[b][:, :], LAYER_ROWS[layer][
                            :, bass.ds(trip * (2 * C) + (2 + b) * C, C)]).then_inc(s_idx[b], 1)
                        if layer > 1 and nxt and not whole(trip, b):
                            select_rel(layer, *nxt, range(AHEAD[layer], ALL_PICKS[layer]))
                        v.wait_ge(s_used[b], n + 1)
                        if layer < 2 and nxt and not whole(trip, b):
                            select(layer, *nxt, range(1, PICKS))
                        if layer == 1:
                            v.wait_ge(s_relu[b], trip + 1)
                        if b or not first(layer, trip):
                            v.wait_ge(s_scan[1 - b], n + b)
                        nc.vector.scalar_tensor_tensor(
                            msgT[b][:, :, 0], msgT[1 - b][:, :, C - 1], same[:, bass.ds(trip * (2 * C) + b * C, 1)],
                            msgT[b][:, :, 0], ALU.mult, ALU.add).then_inc(s_mixed, 1)
                        v.wait_ge(s_mixed, 2 * n + b + 1)
                        v.wait_ge(s_keep, 2 * n + b + 1)
                        for f in range(0, D, KF):
                            block_of = msgT[b][:, f:min(f + KF, D), :].rearrange("p f t -> p (f t)")
                            last = nc.vector.tensor_tensor_scan(
                                block_of, keep[:, 0:min(KF, D - f), :].rearrange("p f t -> p (f t)"), block_of,
                                0.0, ALU.mult, ALU.add)
                        last.then_inc(s_scan[b], 1)
                        if layer == 0:
                            hot(PAIRS, trip, b, dst_lo, dst_hi)
                        if layer < 2 and nxt and following(*nxt):
                            select(layer, *following(*nxt), [0])
                        if layer > 1 and nxt and following(*nxt):
                            select_rel(layer, *following(*nxt), range(AHEAD[layer]))
                        if layer > 1 and nxt:
                            place_rel(layer, *nxt)

                if layer in (0, 3):
                    v.wait_ge(s_wps, 1 if layer == 0 else 2)
                v.wait_ge(s_ramp, max(layer, 1))
                trips(v, body)
                v.wait_ge(s_scan[1], (layer + 1) * PAIRS)
                nc.vector.tensor_copy(tail_sum[:, :], msgT[1][:, :, C - 1]).then_inc(s_tail, 1)

            def degrees():
                v.wait_ge(s_cnt64, 2)
                nc.vector.tensor_copy(deg64[:, :], hist).then_inc(s_deg64, 1)
                v.wait_ge(s_deg, 2)
                link(nc.vector.tensor_copy(deg_in[:, :], deg_ps))
                nc.vector.tensor_scalar(in_clip[:, :], deg_in[:, :], 1.0, None, ALU.max).then_inc(s_clip, 1)
                link(nc.vector.tensor_scalar(has_in[:, :], deg_in[:, :], 1.0, None, ALU.min))
                v.wait_ge(s_clip, 2)
                link(nc.vector.reciprocal(in_inv[:, :], in_clip[:, :]))
                v.wait_ge(s_cum, 1)
                link(nc.vector.tensor_copy(col_tot[:, :], tot_ps))
                link(nc.vector.tensor_tensor_scan(col_cum[:, :], ones[:, 0:COLS], col_tot[:, :], -1.0,
                                                  ALU.mult, ALU.add))
                link(nc.vector.tensor_tensor(col_cum[:, :], col_cum[:, :], col_tot[:, :], ALU.subtract))
                link(nc.vector.tensor_tensor(end_f[:, :], cum_ps, col_cum[:, :], ALU.add))
                link(nc.vector.tensor_scalar(end_f[:, :], end_f[:, :], 0.0, None, ALU.max))
                link(nc.vector.tensor_scalar(end_up[:, :], end_f[:, :], float(E_HALF), float(OVERLAP),
                                             ALU.is_ge, ALU.mult))
                link(nc.vector.tensor_tensor(end_f[:, :], end_f[:, :], end_up[:, :], ALU.add))
                link(nc.vector.scalar_tensor_tensor(end_f[:, :], end_f[:, :], float(P * SLOTS), has_in[:, :],
                                                    ALU.subtract, ALU.mult))
                nc.vector.tensor_scalar(end_i[:, :], end_f[:, :], float(P * SLOTS), None, ALU.add)\
                    .then_inc(s_endi, 1)
                v.wait_ge(s_sqrt, 2)
                link(nc.vector.reciprocal(in_scale[:, :], in_sqrt[:, :]))

            def sum_ends(layer, g):
                q = layer * NG + g
                cols = slice(g * G, (g + 1) * G)
                a = agg[q % 2][:, :]
                v.wait_ge(s_end[g], 16 * G * (layer + 1))
                if q >= 2 and layer < 2:
                    v.wait_ge(s_turn, q - 1)
                if g == 0:
                    v.wait_ge(s_csum, layer + 1)
                ends = ends_sum[:, cols, :].rearrange("p c f -> p (c f)")
                add = nc.vector.tensor_tensor(a, ends, side[:, cols, :].rearrange("p c f -> p (c f)"), ALU.add)
                if layer in (0, 2):
                    link(add)
                    scale = in_scale if layer == 0 else in_inv
                    add = nc.vector.tensor_tensor(cube(a), cube(a), over_cols(scale[:, cols], G), ALU.mult)
                add.then_inc(s_agg, 1)

            def finish(layer, g):
                q = layer * NG + g
                cols = slice(g * G, (g + 1) * G)
                f = feats[:, cols, :]
                a = agg[q % 2][:, :]
                flat = f.rearrange("p c f -> p (c f)")
                if layer < 3:
                    v.wait_ge(s_lin, q + 1)
                if layer in (0, 2):
                    link(nc.vector.tensor_tensor(ta[:, :], lin_ps(q), resid[:, cols, :].rearrange("p c f -> p (c f)"),
                                                 ALU.add))
                if layer == 2:
                    link(nc.vector.tensor_tensor(ta[:, :], ta[:, :], a, ALU.add))
                if layer == 1:
                    link(nc.vector.tensor_tensor(cube(ta[:, :]), cube(lin_ps(q)),
                                                 bias[layer][:, :].unsqueeze(1).broadcast_to([P, G, D]), ALU.add))
                    link(nc.vector.scalar_tensor_tensor(ta[:, :], ta[:, :], 0.0, flat, ALU.max, ALU.add))
                if layer == 3:
                    v.wait_ge(s_agg, q + 1)
                    link(nc.vector.scalar_tensor_tensor(ta[:, :], a, 0.0, flat, ALU.max, ALU.add))
                link(nc.vector.tensor_reduce(row_sum[:, :], cube(ta[:, :]), AX.X, ALU.add))
                link(nc.vector.tensor_scalar(row_mean[:, :], row_sum[:, :], 1.0 / D, None, ALU.mult))
                link(nc.vector.tensor_tensor(cube(tb[:, :]), cube(ta[:, :]), over_cols(row_mean[:, :], G),
                                             ALU.subtract))
                link(nc.vector.tensor_tensor(ta[:, :], tb[:, :], tb[:, :], ALU.mult))
                link(nc.vector.tensor_reduce(row_sq[:, :], cube(ta[:, :]), AX.X, ALU.add))
                nc.vector.tensor_scalar(row_var[:, :], row_sq[:, :], 1.0 / D, LN_EPS, ALU.mult, ALU.add)\
                    .then_inc(s_var, 1)
                v.wait_ge(s_std, q + 1)
                link(nc.vector.reciprocal(row_inv[:, :], row_std[:, :]))
                nc.vector.tensor_tensor(f, cube(tb[:, :]), over_cols(row_inv[:, :], G), ALU.mult).then_inc(s_new, 1)
                v.wait_ge(s_new, q + 1)

            def feature_parts(layer, g):
                q = layer * NG + g
                if q > NG:
                    v.wait_ge(s_xt, q - NG)
                f = feats[:, g * G:(g + 1) * G, :]
                link(split_parts(part_hm[:, :, 0:D], part_hm[:, :, D:2 * D], part_hl[:, :, D:2 * D], f,
                                 cube(ta[:, :])))
                nc.vector.tensor_copy(part_hl[:, :, 0:D], part_hm[:, :, 0:D]).then_inc(s_parts, 1)

            for layer in range(4):
                if layer:
                    stage(layer, 0)
                    stage(layer, 1)
                if layer:
                    split_table(layer, feats)
                if layer:
                    if layer > 1:
                        v.wait_ge(s_yc, halves_before(layer, COLS))
                    nc.vector.memset(keep[:, :, 0], 0.0).then_inc(s_zero, 1)
                if layer in (0, 2):
                    v.wait_ge(s_tparts, layer + 1)
                    nc.vector.tensor_tensor(resid[:, :, :], feats[:, :, :],
                                            bias[layer][:, :].unsqueeze(1).broadcast_to([P, COLS, D]),
                                            ALU.add).then_inc(s_resid, 1)
                chunks(layer)
                if layer in (0, 2):
                    v.wait_ge(s_resid, 1 + layer // 2)
                if layer == 0:
                    degrees()
                if layer == 1:
                    v.wait_ge(s_carry, 2)
                    nc.vector.scalar_tensor_tensor(
                        side[:, :, :].rearrange("p c f -> p (c f)"), feats[:, :, :].rearrange("p c f -> p (c f)"),
                        eps1p[:, 0:1], carry_ps, ALU.mult, ALU.add).then_inc(s_csum, 1)
                    v.wait_ge(s_csum, 2)
                sum_ends(layer, 0)
                for g in range(NG):
                    if g + 1 < NG:
                        sum_ends(layer, g + 1)
                    finish(layer, g)
                    if layer in (1, 2):
                        feature_parts(layer, g)


_INS = ['x', 'src', 'dst', 'edge_attr_64', 'edge_type_16', 'edge_type_32', 'edge_weight', 'edge_weight1',
        'L0_gnn_W', 'L0_gnn_b', 'L1_gnn_W', 'L1_gnn_b', 'L1_gnn_eps', 'L2_gnn_basis', 'L2_gnn_coeff',
        'L2_gnn_self_weight', 'L2_gnn_bias', 'L3_gnn_weight']
_OUTS = [((3125, 64), 'float32')]


def kernel(**inputs):
    import numpy as _np
    import concourse.bacc as _bacc
    from concourse import mybir as _mybir
    from concourse.bass_utils import run_bass_kernel_spmd as _run

    nc = _bacc.Bacc("TRN2", target_bir_lowering=False, num_devices=1)
    arrays, args = {}, []
    for name in _INS:
        a = _np.ascontiguousarray(inputs[name])
        if a.ndim == 0:
            a = a.reshape(1)
        arrays[f"in_{name}_dram"] = a
        args.append(nc.dram_tensor(f"in_{name}_dram", a.shape, _mybir.dt.from_np(a.dtype), kind="ExternalInput").ap())
    for i, (shape, dtype) in enumerate(_OUTS):
        dt = _mybir.dt.from_np(_np.dtype(dtype))
        args.append(nc.dram_tensor(f"out_{i}_dram", shape, dt, kind="ExternalOutput").ap())
    gnn_stack(nc, *args)
    r = _run(nc, [arrays], core_ids=[0])
    got = tuple(r.results[0][f"out_{i}_dram"] for i in range(len(_OUTS)))
    return got[0]
```
